# Optimizing a Trainium2 kernel written in Bass

```python
import numpy as np
import jax
import jax.numpy as jnp

def _softmax(x, axis=-1):
    return jax.nn.softmax(x, axis=axis)

def _gelu(x):
    return jax.nn.gelu(x, approximate=True)

def _silu(x):
    return jax.nn.silu(x)

def _sigmoid(x):
    return jax.nn.sigmoid(x)

def _layernorm(x, axis=-1, eps=1e-05):
    m = jnp.mean(x, axis=axis, keepdims=True)
    v = jnp.var(x, axis=axis, keepdims=True)
    return (x - m) / jnp.sqrt(v + eps)

def _scatter_add(tgt, idx, src, axis=0):
    return tgt.at[idx].add(src)

def _segment_sum(src, seg, n):
    return jax.ops.segment_sum(src, seg, n)
kernel_name = 'mk_adaln_ffn_d1_seqx_r8_82b808'

def setup_inputs(seed: int=0):
    np.random.seed(seed)
    _w = jnp.asarray

    def _rec_inputs():
        import jax
        import jax.numpy as jnp
        _rk = jax.random.key(seed)
        x = -0.0003929 + 0.9999 * jax.random.normal(jax.random.fold_in(_rk, 1), (128, 32, 256), jnp.float32)
        _lenS = 32 - jax.random.randint(jax.random.fold_in(_rk, 7), (128,), 0, max(1, 32 // 4) + 1, jnp.int32)
        _lenS2 = 32 - jax.random.randint(jax.random.fold_in(_rk, 8), (128,), 0, max(1, 32 // 4) + 1, jnp.int32)
        cond_2048 = 0.00782532 + 1.00527 * jax.random.normal(jax.random.fold_in(_rk, 11), (128, 256), jnp.float32)
        return (x, cond_2048)
    x, cond_2048 = _rec_inputs()

    def _L0_cond_setup():
        import jax, jax.numpy as jnp
        import numpy as np
        HEADS = 16
        EPS = 1e-06

        def _rms_norm(x, g):
            xf = x.astype(jnp.float32)
            y = xf * jax.lax.rsqrt(jnp.mean(xf * xf, axis=-1, keepdims=True) + EPS)
            return y.astype(x.dtype) * g
        key = jax.random.key(seed)
        ks = jax.random.split(key, 6)
        b, n, dim, emb_dim = (4, 256, 256, 256)
        d_head = dim // HEADS
        return {'x': jax.random.normal(ks[0], (b, n, dim), jnp.float32), 'emb': jax.random.normal(ks[1], (b, 1, emb_dim), jnp.float32), 'W_emb': jax.random.normal(ks[2], (emb_dim, 2 * dim), jnp.float32) * emb_dim ** (-0.5), 'b_emb': jnp.zeros((2 * dim,), jnp.float32), 'g_norm': jnp.ones((dim,), jnp.float32), 'W_qkv': jax.random.normal(ks[3], (dim, 3 * dim), jnp.float32) * dim ** (-0.5), 'g_q': jnp.ones((d_head,), jnp.float32), 'g_k': jnp.ones((d_head,), jnp.float32), 'W_out': jax.random.normal(ks[4], (dim, dim), jnp.float32) * dim ** (-0.5)}
    _L0_cond_all = _L0_cond_setup()
    _L0_cond_in = {k: v for k, v in _L0_cond_all.items() if k in ('W_emb', 'b_emb', 'g_norm', 'W_qkv', 'g_q', 'g_k', 'W_out')}
    del _L0_cond_all

    def _L0_ffn_setup():
        import jax, jax.numpy as jnp
        import numpy as np
        B_, S, D = (2, 256, 256)
        F_ = 1024
        R = 16
        H = 16
        HD = D // H
        MOD_SCALE = 0.1
        EPS = 1e-06

        def _rmsnorm(x, w):
            v = jnp.mean(x * x, axis=-1, keepdims=True)
            return x * jax.lax.rsqrt(v + EPS) * w

        def _attention(x, Wq, Wk, Wv, Wo):
            b, s, d = x.shape
            q = (x @ Wq.T).reshape(b, s, H, HD)
            k = (x @ Wk.T).reshape(b, s, H, HD)
            v = (x @ Wv.T).reshape(b, s, H, HD)
            scores = jnp.einsum('bqhd,bkhd->bhqk', q, k) / np.sqrt(HD).astype(np.float32)
            causal = jnp.tril(jnp.ones((s, s), bool))
            scores = jnp.where(causal, scores, jnp.finfo(scores.dtype).min)
            probs = jax.nn.softmax(scores, axis=-1)
            out = jnp.einsum('bhqk,bkhd->bqhd', probs, v).reshape(b, s, d)
            return out @ Wo.T
        key = jax.random.key(seed)
        ks = jax.random.split(key, 12)
        sd = 0.02
        return {'hidden_states': jax.random.normal(ks[0], (B_, S, D), jnp.float32), 'ln1_w': jnp.ones((D,), jnp.float32), 'ln2_w': jnp.ones((D,), jnp.float32), 'Wq': jax.random.normal(ks[1], (D, D), jnp.float32) * sd, 'Wk': jax.random.normal(ks[2], (D, D), jnp.float32) * sd, 'Wv': jax.random.normal(ks[3], (D, D), jnp.float32) * sd, 'Wo': jax.random.normal(ks[4], (D, D), jnp.float32) * sd, 'A': jax.random.normal(ks[5], (D, R), jnp.float32) * (0.01 / np.sqrt(D)), 'B': jax.random.normal(ks[6], (R, F_), jnp.float32) * (0.01 / np.sqrt(R)), 'W_in_base': jax.random.normal(ks[7], (F_, D), jnp.float32) * sd, 'W_up_base': jax.random.normal(ks[8], (F_, D), jnp.float32) * sd, 'W_down': jax.random.normal(ks[9], (D, F_), jnp.float32) * sd}
    _L0_ffn_all = _L0_ffn_setup()
    _L0_ffn_in = {k: v for k, v in _L0_ffn_all.items() if k in ('ln1_w', 'ln2_w', 'Wq', 'Wk', 'Wv', 'Wo', 'A', 'B', 'W_in_base', 'W_up_base', 'W_down')}
    del _L0_ffn_all
    return {'x': x, 'cond_2048': cond_2048, 'L0_cond_W_emb': _L0_cond_in['W_emb'], 'L0_cond_b_emb': _L0_cond_in['b_emb'], 'L0_cond_g_norm': _L0_cond_in['g_norm'], 'L0_cond_W_qkv': _L0_cond_in['W_qkv'], 'L0_cond_g_q': _L0_cond_in['g_q'], 'L0_cond_g_k': _L0_cond_in['g_k'], 'L0_cond_W_out': _L0_cond_in['W_out'], 'L0_ffn_ln1_w': _L0_ffn_in['ln1_w'], 'L0_ffn_ln2_w': _L0_ffn_in['ln2_w'], 'L0_ffn_Wq': _L0_ffn_in['Wq'], 'L0_ffn_Wk': _L0_ffn_in['Wk'], 'L0_ffn_Wv': _L0_ffn_in['Wv'], 'L0_ffn_Wo': _L0_ffn_in['Wo'], 'L0_ffn_A': _L0_ffn_in['A'], 'L0_ffn_B': _L0_ffn_in['B'], 'L0_ffn_W_in_base': _L0_ffn_in['W_in_base'], 'L0_ffn_W_up_base': _L0_ffn_in['W_up_base'], 'L0_ffn_W_down': _L0_ffn_in['W_down']}

def reference(x, cond_2048, L0_cond_W_emb, L0_cond_b_emb, L0_cond_g_norm, L0_cond_W_qkv, L0_cond_g_q, L0_cond_g_k, L0_cond_W_out, L0_ffn_ln1_w, L0_ffn_ln2_w, L0_ffn_Wq, L0_ffn_Wk, L0_ffn_Wv, L0_ffn_Wo, L0_ffn_A, L0_ffn_B, L0_ffn_W_in_base, L0_ffn_W_up_base, L0_ffn_W_down):
    import jax
    import jax.numpy as jnp

    def _L0_cond_ref(x, emb, W_emb, b_emb, g_norm, W_qkv, g_q, g_k, W_out):
        import jax, jax.numpy as jnp
        import numpy as np
        HEADS = 16
        EPS = 1e-06

        def _rms_norm(x, g):
            xf = x.astype(jnp.float32)
            y = xf * jax.lax.rsqrt(jnp.mean(xf * xf, axis=-1, keepdims=True) + EPS)
            return y.astype(x.dtype) * g
        b, n, dim = x.shape
        h = HEADS
        d = dim // h
        scale_shift = emb @ W_emb + b_emb
        scale, shift = jnp.split(scale_shift, 2, axis=-1)
        xn = _rms_norm(x, g_norm) * (1.0 + scale) + shift
        qkv = xn @ W_qkv
        qkv = qkv.reshape(b, n, 3, h, d)
        q, k, v = jnp.moveaxis(qkv, 2, 0)
        q = jnp.swapaxes(q, 1, 2)
        k = jnp.swapaxes(k, 1, 2)
        v = jnp.swapaxes(v, 1, 2)
        q = _rms_norm(q, g_q)
        k = _rms_norm(k, g_k)
        logits = jnp.einsum('bhqd,bhkd->bhqk', q, k) * d ** (-0.5)
        attn = jax.nn.softmax(logits, axis=-1)
        o = jnp.einsum('bhqk,bhkd->bhqd', attn, v)
        o = jnp.swapaxes(o, 1, 2).reshape(b, n, dim)
        return o + o @ W_out

    def _L0_ffn_ref(hidden_states, ln1_w, ln2_w, Wq, Wk, Wv, Wo, A, B, W_in_base, W_up_base, W_down):
        import jax, jax.numpy as jnp
        import numpy as np
        B_, S, D = (2, 256, 256)
        F_ = 1024
        R = 16
        H = 16
        HD = D // H
        MOD_SCALE = 0.1
        EPS = 1e-06

        def _rmsnorm(x, w):
            v = jnp.mean(x * x, axis=-1, keepdims=True)
            return x * jax.lax.rsqrt(v + EPS) * w

        def _attention(x, Wq, Wk, Wv, Wo):
            b, s, d = x.shape
            q = (x @ Wq.T).reshape(b, s, H, HD)
            k = (x @ Wk.T).reshape(b, s, H, HD)
            v = (x @ Wv.T).reshape(b, s, H, HD)
            scores = jnp.einsum('bqhd,bkhd->bhqk', q, k) / np.sqrt(HD).astype(np.float32)
            causal = jnp.tril(jnp.ones((s, s), bool))
            scores = jnp.where(causal, scores, jnp.finfo(scores.dtype).min)
            probs = jax.nn.softmax(scores, axis=-1)
            out = jnp.einsum('bhqk,bkhd->bqhd', probs, v).reshape(b, s, d)
            return out @ Wo.T
        residual = hidden_states
        x = _rmsnorm(hidden_states, ln1_w)
        attn = _attention(x, Wq, Wk, Wv, Wo)
        mod = MOD_SCALE * jnp.tanh(attn @ A)
        h = _rmsnorm(residual, ln2_w)
        gate_pre = h @ W_in_base.T + mod * (h @ A) @ B
        gate = jax.nn.silu(gate_pre)
        up = h @ W_up_base.T
        mlp_out = gate * up @ W_down.T
        return residual + mlp_out
    x = x + _L0_ffn_ref(_L0_cond_ref(x, cond_2048[:, None, :], L0_cond_W_emb, L0_cond_b_emb, L0_cond_g_norm, L0_cond_W_qkv, L0_cond_g_q, L0_cond_g_k, L0_cond_W_out), L0_ffn_ln1_w, L0_ffn_ln2_w, L0_ffn_Wq, L0_ffn_Wk, L0_ffn_Wv, L0_ffn_Wo, L0_ffn_A, L0_ffn_B, L0_ffn_W_in_base, L0_ffn_W_up_base, L0_ffn_W_down)
    return x

_drawn_inputs = setup_inputs


def setup_inputs(seed=0):
    import zlib

    import numpy as np

    out = dict(_drawn_inputs(seed))
    spreads = {'L0_cond_b_emb': (0.0, 0.1),
     'L0_cond_g_norm': (1.0, 0.2),
     'L0_cond_g_q': (1.0, 0.2),
     'L0_cond_g_k': (1.0, 0.2),
     'L0_ffn_ln1_w': (1.0, 0.6),
     'L0_ffn_ln2_w': (1.0, 0.6)}
    factors = {'L0_ffn_Wq': 64.0,
     'L0_ffn_Wk': 64.0,
     'L0_ffn_Wv': 64.0,
     'L0_ffn_Wo': 64.0,
     'L0_ffn_A': 64.0,
     'L0_ffn_B': 64.0,
     'L0_ffn_W_in_base': 2.77,
     'L0_ffn_W_up_base': 2.704,
     'L0_ffn_W_down': 2.74}
    for name, (base, spread) in spreads.items():
        noise = np.random.default_rng([zlib.crc32(name.encode()), seed]).standard_normal(out[name].shape)
        drawn = base * np.exp(spread * noise) if base else spread * noise
        out[name] = jnp.asarray(drawn.astype(out[name].dtype))
    for name, factor in factors.items():
        out[name] = (out[name] * factor).astype(out[name].dtype)
    return out
```

```python
from contextlib import ExitStack

import numpy as np

import concourse.bass as bass
from concourse import mybir

ALU = mybir.AluOpType
ACT = mybir.ActivationFunctionType
F32 = mybir.dt.float32
F32R = mybir.dt.float32r
BF16 = mybir.dt.bfloat16
I32 = mybir.dt.int32
AX_X = mybir.AxisListType.X

P = 128
B, S, D = 128, 32, 256
H, HD = 16, 16
FF, R = 1024, 16
KT = D // P
HP = H // 2
TILES = 4
GROUP = TILES * P
GROUPS = B * S // GROUP
SEQS = GROUP // S
FC = FF // P
EPS = 1e-6
RSQRT_GUESS = float(0x5F3759DF)
NEWTON_STEPS = 3


def group_order():
    o = []

    def step(name, i, cost=0.0):
        o.append((name, i, cost))

    for q in range(2):
        step("x_square", 2 * q), step("x_square", 2 * q + 1)
        step("x_rms", q)
        step("x_norm", 2 * q), step("x_norm", 2 * q + 1)
    for t in range(TILES):
        step("x_turn", t, .43)
    for k in range(KT):
        step("x_modulate", k)
    for k in range(KT):
        step("x_split", k)
    for t in range(TILES):
        step("qkv", t, 1.95), step("qkv_out", t), step("qk_squares", t)
        if t % 2:
            step("qk_rms", t // 2)
            step("qk_norm", t - 1), step("qk_norm", t)
        if t == 2:
            step("qk_turn", 0), step("qk_turn", 1)
    step("scores", 0, 1.5), step("shift", 0), step("exp", 0)
    step("scores", 1, 1.5), step("shift", 1), step("exp", 1)
    step("qk_turn", 2)
    step("p_turn", 0)
    step("scores", 2, 1.5), step("shift", 2), step("exp", 2)
    step("qk_turn", 3)
    step("p_turn", 1), step("pv", 0, 1.5)
    step("scores", 3, 1.5), step("shift", 3), step("exp", 3)
    step("p_turn", 2), step("o_turn", 0), step("pv", 1, 1.5)
    step("p_turn", 3), step("o_turn", 1), step("pv", 2, 1.5)
    step("o_turn", 2), step("pv", 3, 1.5), step("o_turn", 3)
    for t in range(TILES):
        step("on_turn", t, .43)
    for k in range(KT):
        step("o_split", k)
    for t in range(TILES):
        step("res", t, .65)
        if t % 2:
            step("res_square", t // 2), step("res_add", t // 2), step("res_rms", t // 2)
            step("res_norm", t - 1), step("res_norm", t)
    for t in range(TILES):
        step("u_turn", t, .43)
    for k in range(KT):
        step("u_split", k)
    step("qkv2", 0, 2.1), step("qkv2_out", 0)
    step("qkv2", 1, 2.1), step("qk_turn", 4), step("qkv2_out", 1)
    step("qkv2", 2, 2.1), step("qk_turn", 5)
    step("qkv2_out", 2)
    step("scores", 4, 1.7), step("shift", 4), step("exp", 4)
    step("qk_turn", 6)
    step("scores", 5, 1.7), step("shift", 5), step("exp", 5)
    step("qkv2", 3, 2.1), step("qkv2_out", 3), step("p_sum", 4), step("p_scale", 4)
    step("scores", 6, 1.7), step("p_turn", 4), step("shift", 6), step("exp", 6)
    step("p_sum", 5), step("p_scale", 5)
    step("pv", 4, 1.5)
    step("qk_turn", 7)
    step("scores", 7, 1.7), step("p_turn", 5), step("shift", 7), step("exp", 7)
    step("p_sum", 6), step("p_scale", 6), step("oa_turn", 0)
    step("pv", 5, 1.5)
    step("p_turn", 6), step("p_sum", 7), step("p_scale", 7), step("oa_turn", 1)
    step("pv", 6, 1.5)
    step("p_turn", 7), step("oa_turn", 2)
    step("pv", 7, 1.5), step("oa_turn", 3)
    step("mod", 0)
    for t in range(TILES):
        step("m_turn", t, .2)
    step("m_out", 0)
    return o


def ffn_order():
    o = []
    for c in range(FC):
        o += [("up", c, 1.3), ("gate", c, 1.5)]
        if c:
            o.append(("gated_split", c - 1, 0.0))
        o.append(("gated", c, 0.0))
    o.append(("gated_split", FC - 1, 0.0))
    for t in range(TILES):
        o += [("down", t, 2.6), ("out", t, 0.0)]
    return o


def merged(attention, filler, ahead, until="u_split", first="gate"):
    out, f = [], 0
    cut = next(i for i, s in enumerate(attention) if s[0] == until)
    split = next((i for i, s in enumerate(filler) if s[0] == "down"), len(filler))
    for a, z, fa, fz, early in ((0, cut, 0, split, ahead), (cut, len(attention), split, len(filler), 0.0)):
        whole = sum(s[2] for s in attention[a:z]) or 1.0
        whole_f = sum(s[2] for s in filler[fa:fz]) or 1.0
        done = done_f = 0.0
        f = fa
        for s in attention[a:z]:
            out.append(("attention",) + s[:2])
            done += s[2]
            while f < fz and done_f / whole_f < min(1.0, done / whole + early) :
                out.append(("ffn",) + filler[f][:2])
                done_f += filler[f][2]
                f += 1
                if done_f >= whole_f and f < fz and filler[f][2] == 0.0:
                    continue
        while f < fz:
            out.append(("ffn",) + filler[f][:2])
            f += 1
    return out


PIECES = [("qkv0", 768), ("qkv1", 768), ("w_out", 512), ("q2", 512), ("k2", 512), ("a2", 32),
          ("in0", 1024), ("in1", 1024), ("up0", 1024), ("up1", 1024), ("down0", 1024), ("down1", 1024),
          ("b", 1024)]


def prologue_order(attention):
    out, n = [], 2
    due = {"qkv_out": 1, "scores": 1, "res": 1, "u_turn": 1, "pv": 1}
    for s in attention:
        out.append(("attention",) + s[:2])
        for _ in range(due.get(s[0], 0)):
            if n < len(PIECES):
                out.append(("weights", "piece", n))
                n += 1
                if n == 6:
                    out.append(("weights", "v2", 0))
    while n < len(PIECES):
        out.append(("weights", "piece", n))
        n += 1
    return out


def bass_adaln_attention_ffn(nc, x, condT, w_emb, b_emb, g_norm, w_qkv, gq, gk, w_out, ln1, ln2,
                             wqT, wkT, wv, wo, a_w, b_w, w_inT, w_upT, w_downT,
                             ident_d, heads_d, causal_d, out):
    xv = x.rearrange("(g q t p) d -> g q p t d", q=2, t=2, p=P)
    outv = out.rearrange("(g t p) d -> g t p d", t=TILES, p=P)

    with ExitStack() as ctx:
        def sb(name, shape, dt=F32):
            return ctx.enter_context(nc.sbuf_tensor(name, shape, dt))

        def sem(name):
            return ctx.enter_context(nc.semaphore(name))

        wqkv = [sb(f"wqkv_{s}", [P, KT, 3 * D], F32R) for s in ("hi", "lo")]
        wres = [sb(f"wres_{s}", [P, KT, D], F32R) for s in ("hi", "lo")]
        wqkv2 = [sb(f"wqkv2_{s}", [P, KT, 3 * D + R], F32R) for s in ("hi", "lo")]
        win = [sb(f"win_{s}", [P, KT, FF], F32R) for s in ("hi", "lo")]
        wup = [sb(f"wup_{s}", [P, KT, FF], F32R) for s in ("hi", "lo")]
        wdn = [sb(f"wdn_{s}", [P, FC, D], F32R) for s in ("hi", "lo")]
        b3 = sb("b3", [96, FF], F32R)
        ident = sb("ident", [P, P])
        identb = sb("identb", [P, P], BF16)
        causal = sb("causal", [P, S])
        maskb = sb("maskb", [P, H, S], BF16)
        heads = sb("heads", [P, 8])
        small = sb("small", [P, 16])
        an = sb("an", [P, KT, R])
        gqk = sb("gqk", [P, D])
        scaleT = sb("scaleT", [P, KT, B])
        shiftT = sb("shiftT", [P, KT, B])

        x_sb = [sb(f"x{q}", [P, 2, D]) for q in range(2)]
        tok = sb("tok", [P, TILES, D])
        xm = sb("xm", [P, KT, GROUP])
        ah = sb("ah", [P, KT, GROUP], F32R)
        al = sb("al", [P, KT, GROUP], F32R)
        uh = sb("uh", [P, KT, GROUP], F32R)
        ul = sb("ul", [P, KT, GROUP], F32R)
        sq = sb("sq", [P, 2, 2 * D])
        qk = sb("qk", [P, TILES, 2 * D])
        vs = sb("vs", [P, TILES, D + R])
        qn = sb("qn", [P, 2, D])
        kp = sb("kp", [P, HP, 2, 2, HD])
        qT = sb("qT", [P, 2, D])
        kT = sb("kT", [P, 2, 2 * D])
        z = sb("z", [P, 2, H, S])
        pT = sb("pT", [P, 2, H * S])
        oq = sb("oq", [P, 2, HP, 4 * HD])
        mx = sb("mx", [P, 2, H])
        rsum = sb("rsum", [P, 2, H])
        rinv = sb("rinv", [P, TILES, H])
        ssx = sb("ssx", [P, TILES])
        rx = sb("rx", [P, TILES])
        ssr = sb("ssr", [P, TILES])
        rr = sb("rr", [P, TILES])
        ssq = sb("ssq", [P, TILES, 2 * H])
        rqk = sb("rqk", [P, TILES, 2 * H])
        nw_a = sb("nw_a", [P, 64])
        nw_y = sb("nw_y", [P, 64])
        nw_t = sb("nw_t", [P, 64])
        oa4 = sb("oa4", [P, TILES, 4 * HD])
        oa = sb("oa", [P, TILES, R])
        th16 = sb("th16", [P, TILES, R])
        m16 = sb("m16", [P, TILES, R])
        mt = sb("mt", [P, TILES, 96])
        mT = sb("mT", [96, GROUP], F32R)
        xres = sb("xres", [P, 2, TILES, D])
        gh = sb("gh", [P, FC, GROUP], F32R)
        gl = sb("gl", [P, FC, GROUP], F32R)
        ffn_work = sb("ffn_work", [P, 2048])
        th = ffn_work[:, 0:GROUP]
        g_up = ffn_work[:, GROUP:3 * GROUP].rearrange("p (c n) -> p c n", c=2)
        outb = ffn_work[:, 3 * GROUP:4 * GROUP].rearrange("p (t d) -> p t d", t=2)
        stage = ffn_work[:, 0:2048].rearrange("p (s n) -> p s n", s=2)
        we = xres[:, 1].rearrange("p t d -> p (t d)").rearrange("p (k n) -> p k n", k=KT)
        wvn = xres[:, 0, 0:2, :]
        won = xres[:, 0, 2:4, :]
        cT = xm[:, 0, 0:KT * B].rearrange("p (k n) -> p k n", k=KT)
        mblk = xres[:, 1, 0, :].rearrange("p (k h r) -> p k h r", k=KT, h=8)
        gq_sb = qk[:, 0, 0:D]
        gk_sb = qk[:, 0, D:2 * D]

        A = [ctx.enter_context(nc.psum_tensor(f"attn_bank{i}", [P, 512], F32)) for i in range(4)]
        Fb = [ctx.enter_context(nc.psum_tensor(f"ffn_bank{i}", [P, 512], F32)) for i in range(4)]

        x_loaded = [sem(f"x_loaded{q}") for q in range(2)]
        out_stored = [sem(f"out_stored{t}") for t in range(TILES)]
        emb_loaded = sem("emb_loaded")
        v2_loaded = sem("v2_loaded")
        piece_loaded = [sem(f"piece_loaded{i}") for i in range(2)]
        piece_split = sem("piece_split")
        piece_hi = sem("piece_hi")
        emb_mm, m_mm, v2_mm = sem("emb_mm"), sem("m_mm"), sem("v2_mm")
        prep, mblk_done = sem("prep"), sem("mblk_done")
        v2_hi = sem("v2_hi")
        pads_zeroed = sem("pads_zeroed")
        x_squared, x_rms_done, x_normed, xT_mm = sem("x_squared"), sem("x_rms_done"), sem("x_normed"), sem("xT_mm")
        x_scaled, x_shifted, xh_done, xl_done = sem("x_scaled"), sem("x_shifted"), sem("xh_done"), sem("xl_done")
        qkv_mm, qk_squared, qkv_copied = sem("qkv_mm"), sem("qk_squared"), sem("qkv_copied")
        qk_summed, qk_rms_done, q_scaled, qk_normed = (sem("qk_summed"), sem("qk_rms_done"), sem("q_scaled"),
                                                       sem("qk_normed"))
        qk_turned, scores_mm, maxed, shifted, exped = (sem("qk_turned"), sem("scores_mm"), sem("maxed"),
                                                       sem("shifted"), sem("exped"))
        summed, inverted, scaled, p_turned, pv_mm = (sem("summed"), sem("inverted"), sem("scaled"),
                                                     sem("p_turned"), sem("pv_mm"))
        o_turned, o_normed, oT_mm, oh_done, ol_done = (sem("o_turned"), sem("o_normed"), sem("oT_mm"),
                                                       sem("oh_done"), sem("ol_done"))
        res_mm, res_squared, xres_done, res_rms_done, u_done = (sem("res_mm"), sem("res_squared"),
                                                                sem("xres_done"), sem("res_rms_done"), sem("u_done"))
        uT_mm, uh_done, ul_done, qkv2_mm, qkv2_copied = (sem("uT_mm"), sem("uh_done"), sem("ul_done"),
                                                         sem("qkv2_mm"), sem("qkv2_copied"))
        oa_turned, oa_summed, oa_tanh, m_done, mT_mm, mT_done = (sem("oa_turned"), sem("oa_summed"), sem("oa_tanh"),
                                                      sem("m_done"), sem("mT_mm"), sem("mT_done"))
        newton, m_chain = sem("newton"), sem("m_chain")
        gate_mm, up_mm, tanh_done, half_gated, gated_done = (sem("gate_mm"), sem("up_mm"), sem("tanh_done"),
                                                             sem("half_gated"), sem("gated_done"))
        gh_done, gl_done, down_mm, out_done = sem("gh_done"), sem("gl_done"), sem("down_mm"), sem("out_done")

        credit = [gated_done, gl_done, down_mm, out_done, *out_stored]

        def wait(eng, s, per_group, g, n):
            if any(s is c for c in credit):
                n += per_group
            if isinstance(g, int):
                if g * per_group + n > 0:
                    eng.wait_ge(s, g * per_group + n)
            else:
                eng.wait_ge(s, g * per_group + n)

        attention = group_order()
        steady = merged(attention, ffn_order(), 0.08)
        first = prologue_order(attention)
        last = [("ffn",) + s[:2] for s in ffn_order()]

        def run(eng, steps, do_attention, do_ffn, do_weights):
            for kind, name, i in first:
                if kind == "attention":
                    do_attention(name, 0, i)
                else:
                    do_weights(name, i)
            with eng.Fori(1, GROUPS) as g:
                for kind, name, i in steps:
                    if kind == "attention":
                        do_attention(name, g, i)
                    else:
                        do_ffn(name, g - 1, i)
            for _, name, i in last:
                do_ffn(name, GROUPS - 1, i)

        piece_names = [n for n, _ in PIECES]

        def piece_parts(n):
            name = piece_names[n]
            st = stage[:, n % 2, 0:PIECES[n][1]]
            if name[:3] == "qkv":
                k = int(name[3])
                return [(st, wqkv[0][:, k, :], wqkv[1][:, k, :], 1.0)]
            if name == "w_out":
                st = st.rearrange("p (k n) -> p k n", k=KT)
                return [(st, wres[0][:, :, :], wres[1][:, :, :], 1.0)]
            if name in ("q2", "k2", "a2"):
                w = R if name == "a2" else D
                lo = {"q2": 0, "k2": D, "a2": 3 * D}[name]
                first_col = {"q2": 12, "k2": 8, "a2": 10}[name]
                st = st.rearrange("p (k n) -> p k n", k=KT)
                return [(st[:, k, :], wqkv2[0][:, k, lo:lo + w], wqkv2[1][:, k, lo:lo + w],
                         small[:, first_col + k:first_col + k + 1]) for k in range(KT)]
            if name[:2] in ("in", "up"):
                k = int(name[2])
                w = win if name[:2] == "in" else wup
                return [(st, w[0][:, k, :], w[1][:, k, :], small[:, 10 + k:11 + k])]
            if name[:4] == "down":
                k = int(name[4])
                st = st.rearrange("p (k n) -> p k n", k=FC // 2)
                sl = slice(k * FC // 2, (k + 1) * FC // 2)
                return [(st, wdn[0][:, sl, :], wdn[1][:, sl, :], 0.5)]
            return []

        def padded(src):
            whole = kp[:, :, :, :, :].rearrange("p a b c d -> p a (b c d)")
            dst = bass.AP(whole.tensor, whole.offset, [whole.ap[0], [4 * HD, HP], [3 * HD, 2], [1, HD]])
            return dst, src.rearrange("p (a b d) -> p a b d", a=HP, b=2)

        def own_head(src):
            return bass.AP(src.tensor, src.offset, [src.ap[0], [4 * HD, HP], [3 * HD, 2], [1, HD]])

        block = ctx.enter_context(nc.Block())

        @block.sync
        def _(sp):
            def load_x(g, q):
                wait(sp, xres_done, 2, g, q - 1)
                src = xv[bass.ds(g, 1), q].rearrange("g p t d -> p (g t) d")
                sp.dma_start(x_sb[q][:, :, :], src).then_inc(x_loaded[q], 16)

            def load_piece(n):
                if n >= 2:
                    sp.wait_ge(piece_split, n - 1)
                name = piece_names[n]
                to = piece_loaded[n % 2]
                dst = stage[:, n % 2, 0:PIECES[n][1]]
                if name == "b":
                    for j in range(3):
                        sp.dma_start(stage[32 * j:32 * j + R, n % 2, :], b_w).then_inc(to, 16)
                    return
                if name[:3] == "qkv":
                    k = int(name[3])
                    src = w_qkv[k * P:(k + 1) * P, :]
                elif name[:2] in ("in", "up"):
                    k = int(name[2])
                    src = (w_inT if name[:2] == "in" else w_upT)[k * P:(k + 1) * P, :]
                elif name[:4] == "down":
                    k = int(name[4])
                    src = w_downT[k * FF // 2:(k + 1) * FF // 2, :].rearrange("(k p) n -> p k n", p=P)
                    dst = dst.rearrange("p (k n) -> p k n", k=FC // 2)
                else:
                    w = {"w_out": w_out, "q2": wqT, "k2": wkT, "a2": a_w}[name]
                    src = w.rearrange("(k p) n -> p k n", p=P)
                    dst = dst.rearrange("p (k n) -> p k n", k=KT)
                sp.dma_start(dst, src).then_inc(to, 16)

            load_x(0, 0)
            load_x(0, 1)
            sp.dma_start(ident[:, :], ident_d).then_inc(emb_loaded, 16)
            sp.dma_start(we, w_emb.rearrange("(k p) n -> p k n", p=P)).then_inc(emb_loaded, 16)
            sp.dma_start(cT, condT.rearrange("(k p) n -> p k n", p=P)).then_inc(emb_loaded, 16)
            for col, v, n in ((0, b_emb, 4), (6, g_norm, 2), (8, ln1, 2), (10, ln2, 2)):
                with nc.allow_non_contiguous_dma(reason="vectors of features onto partitions"):
                    sp.dma_start(small[:, col:col + n], v.rearrange("(k p) -> p k", p=P)).then_inc(emb_loaded, 16)
            sp.dma_start(gq_sb, gq).then_inc(emb_loaded, 16)
            sp.dma_start(gk_sb, gk).then_inc(emb_loaded, 16)
            sp.dma_start(causal[:, :], causal_d).then_inc(emb_loaded, 16)
            load_piece(0)
            load_piece(1)
            sp.dma_start(heads[:, :], heads_d).then_inc(v2_loaded, 16)
            sp.dma_start(won, wo.rearrange("(k p) n -> p k n", p=P)).then_inc(v2_loaded, 16)
            sp.dma_start(wvn, wv.rearrange("(k p) n -> p k n", p=P)).then_inc(v2_loaded, 16)
            sp.dma_start(an[:, :, :], a_w.rearrange("(k p) n -> p k n", p=P)).then_inc(v2_loaded, 16)
            for n in range(2, len(PIECES)):
                load_piece(n)
            load_x(1, 0)
            load_x(1, 1)

            def store(g, t):
                wait(sp, out_done, TILES, g, t + 1)
                dst = outv[bass.ds(g, 1), t].rearrange("g p d -> p (g d)")
                sp.dma_start(dst, outb[:, t % 2, :]).then_inc(out_stored[t], 16)

            with sp.Fori(1, GROUPS - 1) as g:
                load_x(g + 1, 0)
                load_x(g + 1, 1)
                for t in range(TILES):
                    store(g - 1, t)
            for g in (GROUPS - 2, GROUPS - 1):
                for t in range(TILES):
                    store(g, t)
            for t in range(TILES):
                sp.wait_ge(out_stored[t], 16 * (GROUPS + 1))

        @block.tensor
        def _(pe):
            def three_passes(dst, stat, mov, first_mm, last_mm):
                for j, (a, b) in enumerate(((0, 0), (0, 1), (1, 0))):
                    mm = pe.matmul(dst, stat[a], mov[b], start=first_mm and j == 0, stop=last_mm and j == 2)
                return mm

            def token_major(dsts, stat_hi, stat_lo, w, cols, t):
                for k in range(KT):
                    for j, (a, b) in enumerate(((stat_hi, 0), (stat_hi, 1), (stat_lo, 0))):
                        for dst, (c0, c1) in zip(dsts, cols):
                            mm = pe.matmul(dst, a[:, k, t * P:(t + 1) * P], w[b][:, k, c0:c1],
                                           start=(k == 0 and j == 0), stop=(k == KT - 1 and j == 2))
                return mm

            def do_attention(name, g, i):
                t = i
                if name == "x_turn":
                    wait(pe, x_normed, TILES, g, t + 1)
                    if t == 0:
                        wait(pe, mT_done, 1, g, 0)
                        wait(pe, oa_turned, TILES, g, 0)
                    for k in range(KT):
                        mm = pe.transpose(A[k][:, t * P:(t + 1) * P], tok[:, t, k * P:(k + 1) * P], ident[:, :])
                    mm.then_inc(xT_mm, 1)
                elif name == "qkv":
                    if t == 0:
                        wait(pe, xl_done, KT, g, KT)
                        wait(pe, x_scaled, KT, g, KT)
                    elif t == 1:
                        wait(pe, oa_turned, TILES, g, 0)
                    else:
                        wait(pe, qkv_copied, TILES, g, t - 1)
                    if isinstance(g, int) and t == 0:
                        pe.wait_ge(piece_split, 2)
                    pair = 2 * (t % 2)
                    token_major([A[pair][:, :], A[pair + 1][:, 0:D]], ah, al, wqkv, [(0, 512), (512, 768)],
                                t).then_inc(qkv_mm, 1)
                elif name == "scores":
                    n, second = i, i >= TILES
                    t = n % TILES
                    wait(pe, qk_turned, 2 * TILES, g, n + 1)
                    pair_reader = 2 if t < 2 else 3
                    wait(pe, qkv2_copied if second else qkv_copied, TILES, g, pair_reader + 1)
                    if second:
                        pe.matmul(A[t][:, :], identb[:, :], maskb[:, :, :].rearrange("p h s -> p (h s)"),
                                  start=True, stop=False, skip_group_check=True)
                    for hp in range(HP):
                        for b in range(4):
                            rows = slice(32 * b, 32 * b + 32)
                            wide = 32 * (not second and hp + b == 0)
                            dst = slice(32 * b, 32 * b + 32 + wide)
                            mm = pe.matmul(A[t][dst, 64 * hp:64 * hp + 64], qT[rows, n % 2, 32 * hp:32 * hp + 32 + wide],
                                           kT[rows, n % 2, 64 * hp:64 * hp + 64], start=not second, stop=True,
                                           skip_group_check=True)
                    mm.then_inc(scores_mm, 1)
                elif name == "pv":
                    n, second = i, i >= TILES
                    t = n % TILES
                    wait(pe, p_turned, 2 * TILES, g, n + 1)
                    for hp in range(HP):
                        for b in range(4):
                            rows = slice(32 * b, 32 * b + 32)
                            wide = 32 * (hp + b == 0)
                            out_rows = slice(32 * b, 32 * b + 32 + wide)
                            dst = A[t][out_rows, 0:64] if second else A[t][out_rows, 64 * hp:64 * hp + 64]
                            mm = pe.matmul(dst, vs[rows, t, 32 * hp:32 * hp + 32 + wide],
                                           pT[rows, n % 2, 64 * hp:64 * hp + 64],
                                           start=(not second or hp == 0), stop=(not second or hp == HP - 1),
                                           skip_group_check=True)
                    mm.then_inc(pv_mm, 1)
                elif name == "on_turn":
                    wait(pe, o_normed, TILES, g, t + 1)
                    if t == 0:
                        wait(pe, o_turned, TILES, g, 2)
                    for k in range(KT):
                        mm = pe.transpose(A[k][:, t * P:(t + 1) * P], tok[:, t, k * P:(k + 1) * P], ident[:, :])
                    mm.then_inc(oT_mm, 1)
                elif name == "res":
                    if t == 0:
                        wait(pe, ol_done, KT, g, KT)
                        wait(pe, o_turned, TILES, g, TILES)
                        if isinstance(g, int):
                            pe.wait_ge(piece_split, 3)
                    dst = A[2 + t // 2][:, (t % 2) * D:(t % 2 + 1) * D]
                    token_major([dst], ah, al, wres, [(0, D)], t).then_inc(res_mm, 1)
                elif name == "u_turn":
                    wait(pe, u_done, TILES, g, t + 1)
                    if t == 0:
                        wait(pe, ol_done, KT, g, KT)
                    for k in range(KT):
                        mm = pe.transpose(A[k][:, t * P:(t + 1) * P], tok[:, t, k * P:(k + 1) * P], ident[:, :])
                    mm.then_inc(uT_mm, 1)
                elif name == "qkv2":
                    if t == 0:
                        wait(pe, ul_done, KT, g, KT)
                        if isinstance(g, int):
                            pe.wait_ge(piece_split, 6)
                            pe.wait_ge(v2_hi, 2)
                    elif t == 1:
                        wait(pe, u_done, TILES, g, TILES)
                    else:
                        wait(pe, qkv2_copied, TILES, g, t - 1)
                    pair = 2 * (t % 2)
                    token_major([A[pair][:, :], A[pair + 1][:, 0:D + R]], uh, ul, wqkv2,
                                [(0, 512), (512, 768 + R)], t).then_inc(qkv2_mm, 1)
                elif name == "m_turn":
                    if t == 0:
                        wait(pe, m_done, 1, g, 1)
                        wait(pe, oa_turned, TILES, g, TILES)
                    pe.transpose(A[0][0:96, t * P:(t + 1) * P], mt[:, t, :], ident[:, :]).then_inc(mT_mm, 1)

            def do_ffn(name, g, i):
                c = i
                if name in ("gate", "up"):
                    bank = Fb[2 * (c % 2) + (name == "up")]
                    w = win if name == "gate" else wup
                    if c >= 2:
                        wait(pe, gated_done, FC, g, c - 1)
                    elif name == "up":
                        wait(pe, out_done, TILES, g, 0)
                    fs = slice(c * P, (c + 1) * P)
                    for k in range(KT):
                        mm = three_passes(bank[:, :], (w[0][:, k, fs], w[1][:, k, fs]), (uh[:, k, :], ul[:, k, :]),
                                          k == 0, name == "up" and k == KT - 1)
                    if name == "gate":
                        if c == 0:
                            wait(pe, mT_done, 1, g, 1)
                        mm = pe.matmul(bank[:, :], b3[:, c * P:(c + 1) * P], mT[:, :], start=False, stop=True)
                        mm.then_inc(gate_mm, 1)
                    else:
                        mm.then_inc(up_mm, 1)
                elif name == "down":
                    t = i
                    if t == 0:
                        wait(pe, gl_done, FC, g, FC)
                    for c in range(FC):
                        mm = three_passes(Fb[t][:, 0:D], (gh[:, c, t * P:(t + 1) * P], gl[:, c, t * P:(t + 1) * P]),
                                          (wdn[0][:, c, :], wdn[1][:, c, :]), c == 0, c == FC - 1)
                    mm.then_inc(down_mm, 1)

            def do_weights(name, n):
                if name == "piece" and piece_names[n] == "w_out":
                    pe.wait_ge(v2_loaded, 64)
                    for m in range(KT):
                        for k in range(KT):
                            mm = pe.matmul(Fb[1][:, m * R:(m + 1) * R], won[:, k, m * P:(m + 1) * P], an[:, k, :],
                                           start=(k == 0), stop=(k == KT - 1))
                    mm.then_inc(m_mm, 1)
                elif name == "v2":
                    pe.wait_ge(mblk_done, 1)
                    for f in range(KT):
                        for m in range(KT):
                            mm = pe.matmul(Fb[2][:, f * D + m * P:f * D + (m + 1) * P],
                                           wvn[:, m, f * P:(f + 1) * P],
                                           mblk[:, m, :, :].rearrange("p h r -> p (h r)"), start=True, stop=True)
                    mm.then_inc(v2_mm, 1)

            pe.wait_ge(emb_loaded, 16 * 10)
            for m in range(4):
                for k in range(KT):
                    mm = pe.matmul(Fb[0][:, m * B:(m + 1) * B], we[:, k, m * P:(m + 1) * P], cT[:, k, :],
                                   start=(k == 0), stop=(k == KT - 1))
                if m == 0:
                    mm.then_inc(down_mm, TILES)
            mm.then_inc(emb_mm, 1)
            run(pe, steady, do_attention, do_ffn, do_weights)

        @block.scalar
        def _(act):
            def do_attention(name, g, i):
                t = i
                if name == "x_square":
                    wait(act, x_loaded[t // 2], 16, g, 16)
                    wait(act, uT_mm, TILES, g, t - 3)
                    act.activation(tok[:, t, :], x_sb[t // 2][:, t % 2, :], ACT.Square,
                                   accum_out=ssx[:, t:t + 1]).then_inc(x_squared, 1)
                elif name == "x_norm":
                    wait(act, x_rms_done, 2, g, t // 2 + 1)
                    act.activation(tok[:, t, :], x_sb[t // 2][:, t % 2, :], ACT.Copy,
                                   scale=rx[:, t:t + 1]).then_inc(x_normed, 1)
                elif name == "x_split":
                    k = i
                    wait(act, x_shifted, KT, g, k + 1)
                    wait(act, res_mm, TILES, g, 0)
                    act.activation(ah[:, k, :], xm[:, k, :], ACT.Copy).then_inc(xh_done, 1)
                elif name == "qkv_out":
                    pair = 2 * (t % 2)
                    wait(act, qkv_mm, TILES, g, t + 1)
                    wait(act, qk_summed, TILES, g, t - 1)
                    act.activation(sq[:, t % 2, :], A[pair][:, :], ACT.Square).then_inc(qk_squared, 1)
                    wait(act, qk_normed, TILES, g, t - 3)
                    act.activation(qk[:, t, :], A[pair][:, :], ACT.Copy)
                    wait(act, pv_mm, 2 * TILES, g, t - 3)
                    act.activation(vs[:, t, 0:D], A[pair + 1][:, 0:D], ACT.Copy).then_inc(qkv_copied, 1)
                elif name == "exp":
                    wait(act, shifted, 2 * TILES, g, i + 1)
                    act.activation(z[:, i % 2], z[:, i % 2], ACT.Exp).then_inc(exped, 1)
                elif name == "o_split":
                    k = i
                    wait(act, oT_mm, TILES, g, TILES)
                    wait(act, qkv_mm, TILES, g, TILES)
                    act.activation(ah[:, k, :], A[k][:, :], ACT.Copy).then_inc(oh_done, 1)
                elif name == "res_square":
                    for t in (2 * i, 2 * i + 1):
                        wait(act, res_mm, TILES, g, 2 * i + 2)
                        act.activation(tok[:, t, :], A[2 + i][:, (t % 2) * D:(t % 2 + 1) * D], ACT.Square,
                                       accum_out=ssr[:, t:t + 1]).then_inc(res_squared, 1)
                elif name == "res_norm":
                    wait(act, res_rms_done, 2, g, t // 2 + 1)
                    act.activation(tok[:, t, :], A[2 + t // 2][:, (t % 2) * D:(t % 2 + 1) * D], ACT.Copy,
                                   scale=rr[:, t:t + 1]).then_inc(u_done, 1)
                elif name == "u_split":
                    k = i
                    wait(act, uT_mm, TILES, g, TILES)
                    wait(act, gate_mm, FC, g, 0)
                    act.activation(uh[:, k, :], A[k][:, :], ACT.Copy).then_inc(uh_done, 1)
                elif name == "qkv2_out":
                    n = TILES + t
                    pair = 2 * (t % 2)
                    wait(act, qkv2_mm, TILES, g, t + 1)
                    wait(act, qk_turned, 2 * TILES, g, n - 1)
                    act.activation(qn[:, n % 2, :], A[pair][:, 0:D], ACT.Copy)
                    wait(act, qk_turned, 2 * TILES, g, n)
                    kdst, ksrc = padded(A[pair][:, D:2 * D])
                    act.activation(kdst, ksrc, ACT.Copy)
                    wait(act, pv_mm, 2 * TILES, g, t + 1)
                    act.activation(vs[:, t, :], A[pair + 1][:, 0:D + R], ACT.Copy).then_inc(qkv2_copied, 1)
                elif name == "mod":
                    wait(act, oa_summed, TILES, g, TILES)
                    act.activation(th16[:, :, :], oa[:, :, :], ACT.Tanh).then_inc(oa_tanh, 1)
                elif name == "m_out":
                    wait(act, mT_mm, TILES, g, TILES)
                    wait(act, gate_mm, FC, g, 0)
                    act.activation(mT[:, :], A[0][0:96, :], ACT.Copy).then_inc(mT_done, 1)

            def do_ffn(name, g, i):
                c = i
                if name == "gate":
                    wait(act, gate_mm, FC, g, c + 1)
                    wait(act, gated_done, FC, g, c)
                    act.activation(th, Fb[2 * (c % 2)][:, :], ACT.Tanh, scale=0.5).then_inc(tanh_done, 1)
                elif name == "gated_split":
                    wait(act, gated_done, FC, g, c + 1)
                    wait(act, down_mm, TILES, g, 0)
                    act.activation(gh[:, c, :], g_up[:, c % 2, :], ACT.Copy).then_inc(gh_done, 1)

            def do_weights(name, n):
                if name == "v2":
                    act.wait_ge(v2_mm, 1)
                    for k in range(KT):
                        hi = act.activation(wqkv2[0][:, k, 512:768], Fb[2][:, k * D:(k + 1) * D], ACT.Copy,
                                            scale=small[:, 8 + k:9 + k])
                    hi.then_inc(v2_hi, 1)
                    return
                act.wait_ge(piece_loaded[n % 2], 16 * (n // 2 + 1))
                if piece_names[n] == "w_out":
                    act.wait_ge(prep, 3)
                hi = None
                for st, hi_ap, _, scale in piece_parts(n):
                    hi = act.activation(hi_ap, st, ACT.Copy, scale=scale)
                if hi is not None:
                    hi.then_inc(piece_hi, 1)

            do_weights("piece", 0)
            do_weights("piece", 1)
            act.wait_ge(prep, 2)
            run(act, steady, do_attention, do_ffn, do_weights)

        @block.vector
        def _(dve):
            count = {"newton": 0, "per_group": 0}

            def rsqrt(dst, src, n, g, signal):
                w = dst.shape[-1] if len(dst.shape) == 2 else dst.shape[-1] * dst.shape[-2]
                a, y, u = nw_a[:, 0:w], nw_y[:, 0:w], nw_t[:, 0:w]
                base = g * count["per_group"]

                def then(ins):
                    count["newton"] += 1
                    ins.then_inc(newton, 1)
                    dve.wait_ge(newton, base + count["newton"])

                then(dve.tensor_scalar(a, src, 1.0 / n, EPS, ALU.mult, ALU.add))
                then(dve.tensor_scalar(y.bitcast(I32), a.bitcast(I32), 1, None, ALU.arith_shift_right))
                then(dve.tensor_scalar(y.bitcast(I32), y.bitcast(I32), -1, RSQRT_GUESS, ALU.mult, ALU.add))
                for s in range(NEWTON_STEPS):
                    then(dve.scalar_tensor_tensor(out=u, in0=y, scalar=-0.5, in1=y, op0=ALU.mult, op1=ALU.mult))
                    then(dve.tensor_tensor(u, u, a, ALU.mult))
                    if s < NEWTON_STEPS - 1:
                        then(dve.scalar_tensor_tensor(out=y, in0=u, scalar=1.5, in1=y, op0=ALU.add, op1=ALU.mult))
                dve.scalar_tensor_tensor(out=dst, in0=u, scalar=1.5, in1=y, op0=ALU.add,
                                         op1=ALU.mult).then_inc(signal, 1)

            def do_attention(name, g, i):
                t = i
                if name == "x_square" and i == 0:
                    count["newton"] = 0
                if name == "x_rms":
                    wait(dve, x_squared, TILES, g, 2 * i + 2)
                    rsqrt(rx[:, 2 * i:2 * i + 2], ssx[:, 2 * i:2 * i + 2], D, g, x_rms_done)
                elif name == "x_modulate":
                    k = i
                    wait(dve, xT_mm, TILES, g, TILES)
                    wait(dve, xh_done, KT, g, k - 1)
                    xmv = xm[:, k, :].rearrange("p (b s) -> p b s", s=S)
                    sc = scaleT[:, k, bass.ds(g * SEQS, SEQS)].unsqueeze(2).to_broadcast([P, SEQS, S])
                    dve.tensor_tensor(xmv, A[k][:, :].rearrange("p (b s) -> p b s", s=S), sc,
                                      ALU.mult).then_inc(x_scaled, 1)
                elif name == "x_split":
                    k = i
                    wait(dve, xh_done, KT, g, k + 1)
                    dve.tensor_tensor(al[:, k, :], xm[:, k, :], ah[:, k, :].bitcast(F32),
                                      ALU.subtract).then_inc(xl_done, 1)
                elif name == "qk_squares":
                    wait(dve, qk_squared, TILES, g, t + 1)
                    wait(dve, qk_rms_done, 2, g, t // 2 - 1)
                    dve.tensor_reduce(ssq[:, t, :], sq[:, t % 2, :].rearrange("p (h d) -> p h d", d=HD), AX_X,
                                      ALU.add).then_inc(qk_summed, 1)
                elif name == "qk_rms":
                    wait(dve, qk_summed, TILES, g, 2 * i + 2)
                    wait(dve, qk_normed, TILES, g, 2 * i - 2)
                    rsqrt(rqk[:, 2 * i:2 * i + 2, :].rearrange("p t h -> p (t h)"),
                          ssq[:, 2 * i:2 * i + 2, :].rearrange("p t h -> p (t h)"), HD, g, qk_rms_done)
                elif name == "qk_turn":
                    n = i
                    if n < TILES:
                        wait(dve, qk_normed, TILES, g, n + 1)
                    else:
                        wait(dve, qkv2_copied, TILES, g, n - TILES + 1)
                    wait(dve, scores_mm, 2 * TILES, g, n - 1)
                    dve.transpose(qT[:, n % 2, :], qn[:, n % 2, :])
                    dve.transpose(kT[:, n % 2, :],
                                  kp[:, :, :, :, :].rearrange("p a b c d -> p (a b c d)")).then_inc(qk_turned, 1)
                elif name == "shift":
                    n, t = i, i % TILES
                    wait(dve, scores_mm, 2 * TILES, g, n + 1)
                    sc = A[t][:, :].rearrange("p (h s) -> p h s", s=S)
                    dve.tensor_reduce(mx[:, n % 2, :], sc, AX_X, ALU.max).then_inc(maxed, 1)
                    wait(dve, maxed, 2 * TILES, g, n + 1)
                    wait(dve, p_turned, 2 * TILES, g, n - 1)
                    dve.tensor_tensor(z[:, n % 2], sc, mx[:, n % 2, :].unsqueeze(2).to_broadcast([P, H, S]),
                                      ALU.subtract).then_inc(shifted, 1)
                elif name in ("p_sum", "p_turn"):
                    n, t = i, i % TILES
                    if name == "p_sum" or n < TILES:
                        wait(dve, exped, 2 * TILES, g, n + 1)
                        wait(dve, inverted, 2 * TILES, g, n)
                        dve.tensor_reduce(rsum[:, n % 2, :], z[:, n % 2], AX_X, ALU.add).then_inc(summed, 1)
                        wait(dve, summed, 2 * TILES, g, n + 1)
                        wait(dve, o_normed if n >= TILES else scaled, TILES, g, t + 1 if n >= TILES else t - 3)
                        dve.reciprocal(rinv[:, t, :], rsum[:, n % 2, :]).then_inc(inverted, 1)
                    if name == "p_turn":
                        if n >= TILES:
                            wait(dve, scaled, TILES, g, t + 1)
                        wait(dve, pv_mm, 2 * TILES, g, n - 1)
                        dve.transpose(pT[:, n % 2, :],
                                      z[:, n % 2].rearrange("p h s -> p (h s)")).then_inc(p_turned, 1)
                elif name == "o_turn":
                    wait(dve, pv_mm, 2 * TILES, g, t + 1)
                    wait(dve, o_normed, TILES, g, t - 1)
                    dve.transpose(oq[:, t % 2].rearrange("p a b -> p (a b)"), A[t][:, :]).then_inc(o_turned, 1)
                elif name == "o_split":
                    k = i
                    wait(dve, oh_done, KT, g, k + 1)
                    dve.tensor_tensor(al[:, k, :], A[k][:, :], ah[:, k, :].bitcast(F32),
                                      ALU.subtract).then_inc(ol_done, 1)
                elif name == "res_add":
                    wait(dve, res_squared, TILES, g, 2 * i + 2)
                    wait(dve, out_done, TILES, g, -TILES)
                    dst = xres[:, bass.ds(g % 2, 1), 2 * i:2 * i + 2, :].rearrange("p g t d -> p (g t) d")
                    dve.tensor_tensor(dst, A[2 + i][:, :].rearrange("p (t d) -> p t d", t=2), x_sb[i][:, :, :],
                                      ALU.add).then_inc(xres_done, 1)
                elif name == "res_rms":
                    rsqrt(rr[:, 2 * i:2 * i + 2], ssr[:, 2 * i:2 * i + 2], D, g, res_rms_done)
                elif name == "u_split":
                    k = i
                    wait(dve, uh_done, KT, g, k + 1)
                    dve.tensor_tensor(ul[:, k, :], A[k][:, :], uh[:, k, :].bitcast(F32),
                                      ALU.subtract).then_inc(ul_done, 1)
                elif name == "oa_turn":
                    wait(dve, pv_mm, 2 * TILES, g, TILES + t + 1)
                    dve.transpose(oa4[:, t, :], A[t][:, 0:64]).then_inc(oa_turned, 1)
                    wait(dve, oa_turned, TILES, g, t + 1)
                    ins = dve.tensor_tensor(oa[:, t, :], oa4[:, t, 0:HD], oa4[:, t, 3 * HD:4 * HD], ALU.add)
                    ins.then_inc(oa_summed, 1)
                elif name == "mod":
                    wait(dve, oa_tanh, 1, g, 1)
                    wait(dve, mT_mm, TILES, g, 0)
                    dve.scalar_tensor_tensor(out=m16[:, :, :], in0=th16[:, :, :], scalar=0.1,
                                             in1=vs[:, :, D:D + R], op0=ALU.mult, op1=ALU.mult).then_inc(m_chain, 1)
                    wait(dve, m_chain, 2, g, 1)
                    dve.tensor_copy(mt[:, :, 0:R].bitcast(F32R), m16[:, :, :])
                    dve.tensor_copy(mt[:, :, 64:64 + R].bitcast(F32R), m16[:, :, :]).then_inc(m_chain, 1)
                    wait(dve, m_chain, 2, g, 2)
                    dve.tensor_tensor(mt[:, :, 32:32 + R], m16[:, :, :], mt[:, :, 64:64 + R],
                                      ALU.subtract).then_inc(m_done, 1)
                elif name == "m_out":
                    if isinstance(g, int):
                        count["per_group"] = count["newton"]

            def do_ffn(name, g, i):
                c = i
                if name == "gated":
                    wait(dve, tanh_done, FC, g, c + 1)
                    dve.scalar_tensor_tensor(out=th, in0=th, scalar=1.0, in1=Fb[2 * (c % 2)][:, :], op0=ALU.add,
                                             op1=ALU.mult).then_inc(half_gated, 1)
                    wait(dve, half_gated, FC, g, c + 1)
                    wait(dve, up_mm, FC, g, c + 1)
                    wait(dve, gl_done, FC, g, max(c - 1, 0))
                    dve.tensor_tensor(g_up[:, c % 2, :], th, Fb[2 * (c % 2) + 1][:, :],
                                      ALU.mult).then_inc(gated_done, 1)
                elif name == "out":
                    t = i
                    wait(dve, down_mm, TILES, g, t + 1)
                    if t < 2:
                        wait(dve, out_stored[t + 2], 16, g, 0)
                    else:
                        wait(dve, out_stored[t - 2], 16, g, 16)
                    wait(dve, xres_done, 2, g, 2)
                    src = xres[:, bass.ds(g % 2, 1), t, :].rearrange("p g d -> p (g d)")
                    dve.tensor_tensor(outb[:, t % 2, :], Fb[t][:, 0:D], src, ALU.add).then_inc(out_done, 1)

            def do_weights(name, n):
                if name == "v2":
                    dve.wait_ge(v2_hi, 1)
                    for k in range(KT):
                        lo = dve.scalar_tensor_tensor(out=wqkv2[1][:, k, 512:768], in0=Fb[2][:, k * D:(k + 1) * D],
                                                      scalar=small[:, 8 + k:9 + k],
                                                      in1=wqkv2[0][:, k, 512:768].bitcast(F32),
                                                      op0=ALU.mult, op1=ALU.subtract)
                    lo.then_inc(v2_hi, 1)
                    return
                name = piece_names[n]
                if name == "b":
                    dve.wait_ge(piece_loaded[n % 2], 16 * (n // 2 + 3))
                    dve.wait_ge(pads_zeroed, 2)
                    for j in range(3):
                        rows = slice(32 * j, 32 * j + R)
                        ins = dve.tensor_copy(b3[rows, :], stage[rows, n % 2, :])
                    ins.then_inc(prep, 1)
                    dve.wait_ge(prep, 4)
                    dve.tensor_tensor(b3[64:64 + R, :], stage[64:64 + R, n % 2, :], b3[64:64 + R, :].bitcast(F32),
                                      ALU.subtract).then_inc(piece_split, 1)
                    return
                if name == "w_out":
                    dve.wait_ge(m_mm, 1)
                    for m in range(KT):
                        mb = dve.tensor_tensor(mblk[:, m], Fb[1][:, m * R:(m + 1) * R].unsqueeze(1).to_broadcast([P, 8, R]),
                                               heads[:, :].unsqueeze(2).to_broadcast([P, 8, R]), ALU.mult)
                    mb.then_inc(mblk_done, 1)
                    dve.wait_ge(piece_loaded[n % 2], 16 * (n // 2 + 1))
                    for k in range(KT):
                        seg = stage[:, n % 2, k * D + k * P:k * D + (k + 1) * P]
                        ins = dve.tensor_tensor(seg, seg, ident[:, :], ALU.add)
                    ins.then_inc(prep, 1)
                dve.wait_ge(piece_hi, n + 1)
                parts = piece_parts(n)
                for j, (st, hi_ap, lo_ap, scale) in enumerate(parts):
                    ins = dve.scalar_tensor_tensor(out=lo_ap, in0=st, scalar=scale, in1=hi_ap.bitcast(F32),
                                                   op0=ALU.mult, op1=ALU.subtract)
                ins.then_inc(piece_split, 1)

            dve.memset(kp[:, :, :, :, :], 0.0).then_inc(gated_done, FC)
            for t in range(TILES):
                dve.memset(mx[:, 0, t:t + 1], 0.0).then_inc(out_stored[t], 16)
            dve.memset(mx[:, 0, TILES:TILES + 1], 0.0).then_inc(out_done, TILES)
            dve.memset(mt[:, :, :], 0.0).then_inc(pads_zeroed, 1)
            dve.memset(b3[:, :].bitcast(F32), 0.0).then_inc(pads_zeroed, 1)
            dve.wait_ge(emb_loaded, 16 * 10)
            dve.tensor_scalar(small[:, 12:14], small[:, 8:10], 0.25, None, ALU.mult)
            dve.tensor_scalar(small[:, 4:6], small[:, 0:2], 1.0, None, ALU.add).then_inc(prep, 1)
            dve.tensor_copy(identb[:, :], ident[:, :])
            dve.tensor_copy(maskb[:, :, :], causal[:, :].unsqueeze(1).to_broadcast([P, H, S]))
            dve.scalar_tensor_tensor(out=gqk[:, :], in0=gq_sb, scalar=float(HD) ** -0.5, in1=gk_sb,
                                     op0=ALU.mult, op1=ALU.mult).then_inc(prep, 1)
            dve.wait_ge(emb_mm, 1)
            dve.wait_ge(prep, 2)
            for k in range(KT):
                dve.tensor_scalar(scaleT[:, k, :], Fb[0][:, k * B:(k + 1) * B], small[:, 4 + k:5 + k],
                                  small[:, 6 + k:7 + k], ALU.add, ALU.mult)
                ins = dve.tensor_scalar(shiftT[:, k, :], Fb[0][:, (2 + k) * B:(3 + k) * B], small[:, 2 + k:3 + k],
                                        None, ALU.add)
            ins.then_inc(pads_zeroed, 1)
            do_weights("piece", 0)
            do_weights("piece", 1)
            run(dve, steady, do_attention, do_ffn, do_weights)

        @block.gpsimd
        def _(pool):
            def do_attention(name, g, i):
                t = i
                if name == "x_modulate":
                    k = i
                    wait(pool, x_scaled, KT, g, k + 1)
                    xmv = xm[:, k, :].rearrange("p (b s) -> p b s", s=S)
                    sh = shiftT[:, k, bass.ds(g * SEQS, SEQS)].unsqueeze(2).to_broadcast([P, SEQS, S])
                    pool.tensor_tensor(xmv, xmv, sh, ALU.add).then_inc(x_shifted, 1)
                elif name == "qk_norm":
                    wait(pool, qkv_copied, TILES, g, t + 1)
                    wait(pool, qk_rms_done, 2, g, t // 2 + 1)
                    pool.tensor_tensor(qk[:, t, 0:D], qk[:, t, 0:D], gqk[:, :], ALU.mult).then_inc(q_scaled, 1)
                    wait(pool, q_scaled, TILES, g, t + 1)
                    wait(pool, qk_turned, 2 * TILES, g, t)
                    pool.tensor_tensor(qn[:, t % 2, :].rearrange("p (h d) -> p h d", d=HD),
                                       qk[:, t, 0:D].rearrange("p (h d) -> p h d", d=HD),
                                       rqk[:, t, 0:H].unsqueeze(2).to_broadcast([P, H, HD]), ALU.mult)
                    kdst, ksrc = padded(qk[:, t, D:2 * D])
                    rk = rqk[:, t, H:2 * H].rearrange("p (a b) -> p a b", a=HP).unsqueeze(3)
                    pool.tensor_tensor(kdst, ksrc, rk.to_broadcast([P, HP, 2, HD]), ALU.mult).then_inc(qk_normed, 1)
                elif name == "o_turn":
                    wait(pool, o_turned, TILES, g, t + 1)
                    wait(pool, inverted, 2 * TILES, g, t + 1)
                    wait(pool, xT_mm, TILES, g, t + 1)
                    ri = rinv[:, t, :].rearrange("p (a b) -> p a b", a=HP).unsqueeze(3)
                    pool.tensor_tensor(tok[:, t, :].rearrange("p (a b d) -> p a b d", a=HP, b=2),
                                       own_head(oq[:, t % 2]), ri.to_broadcast([P, HP, 2, HD]),
                                       ALU.mult).then_inc(o_normed, 1)
                elif name == "p_scale":
                    n, t = i, i % TILES
                    wait(pool, inverted, 2 * TILES, g, n + 1)
                    pool.tensor_tensor(z[:, n % 2], z[:, n % 2], rinv[:, t, :].unsqueeze(2).to_broadcast([P, H, S]),
                                       ALU.mult).then_inc(scaled, 1)

            def do_ffn(name, g, i):
                c = i
                if name == "gated_split":
                    wait(pool, gh_done, FC, g, c + 1)
                    pool.tensor_tensor(gl[:, c, :], g_up[:, c % 2, :], gh[:, c, :].bitcast(F32),
                                       ALU.subtract).then_inc(gl_done, 1)

            pool.memset(rsum[:, 0, 0:1], 0.0).then_inc(gl_done, FC)
            pool.wait_ge(pads_zeroed, 3)
            run(pool, steady, do_attention, do_ffn, lambda name, n: None)


def kernel(**inputs):
    import concourse.bacc as _bacc
    from concourse.bass_utils import run_bass_kernel_spmd as _run

    i = {k: np.asarray(v) for k, v in inputs.items()}
    q = np.arange(P) % S
    heads = (np.arange(P)[:, None] // HD == np.arange(8)[None, :]).astype(np.float32)
    causal = np.where(np.arange(S)[None, :] <= q[:, None], 0.0, -3.0e38).astype(np.float32)
    arrays = {
        "x": i["x"].reshape(B * S, D),
        "condT": i["cond_2048"].T,
        "w_emb": i["L0_cond_W_emb"],
        "b_emb": i["L0_cond_b_emb"],
        "g_norm": i["L0_cond_g_norm"],
        "w_qkv": i["L0_cond_W_qkv"],
        "gq": np.tile(i["L0_cond_g_q"], (P, H)),
        "gk": np.tile(i["L0_cond_g_k"], (P, H)),
        "w_out": i["L0_cond_W_out"],
        "ln1": i["L0_ffn_ln1_w"],
        "ln2": i["L0_ffn_ln2_w"],
        "wqT": i["L0_ffn_Wq"].T,
        "wkT": i["L0_ffn_Wk"].T,
        "wv": i["L0_ffn_Wv"],
        "wo": i["L0_ffn_Wo"],
        "a_w": i["L0_ffn_A"],
        "b_w": i["L0_ffn_B"],
        "w_inT": i["L0_ffn_W_in_base"].T,
        "w_upT": i["L0_ffn_W_up_base"].T,
        "w_downT": i["L0_ffn_W_down"].T,
        "ident": np.eye(P, dtype=np.float32),
        "heads": heads,
        "causal": causal,
    }
    nc = _bacc.Bacc("TRN2", target_bir_lowering=False, num_devices=1)
    sent, args = {}, []
    for name, a in arrays.items():
        a = np.ascontiguousarray(a)
        sent[f"in_{name}"] = a
        args.append(nc.dram_tensor(f"in_{name}", a.shape, mybir.dt.from_np(a.dtype), kind="ExternalInput").ap())
    args.append(nc.dram_tensor("out_0", (B * S, D), F32, kind="ExternalOutput").ap())
    bass_adaln_attention_ffn(nc, *args)
    r = _run(nc, [sent], core_ids=[0])
    return r.results[0]["out_0"].reshape(B, S, D)
```

```python
from contextlib import ExitStack

import numpy as np

import concourse.bass as bass
from concourse import mybir

ALU = mybir.AluOpType
ACT = mybir.ActivationFunctionType
F32 = mybir.dt.float32
F32R = mybir.dt.float32r
BF16 = mybir.dt.bfloat16
I32 = mybir.dt.int32
AX_X = mybir.AxisListType.X

P = 128
B, S, D = 128, 32, 256
H, HD = 16, 16
FF, R = 1024, 16
KT = D // P
HP = H // 2
TILES = 4
GROUP = TILES * P
GROUPS = B * S // GROUP
SEQS = GROUP // S
FC = FF // P
EPS = 1e-6
RSQRT_GUESS = float(0x5F3759DF)
NEWTON_STEPS = 3


def x_order():
    o = []
    for q in range(2):
        o += [("x_square", 2 * q), ("x_square", 2 * q + 1), ("x_rms", q), ("x_norm", 2 * q), ("x_norm", 2 * q + 1)]
    for q in range(2):
        o += [("x_turn", 2 * q), ("x_turn", 2 * q + 1), ("x_modulate", q), ("x_split", q)]
    return o


ATTENTION = [
    ("qkv", 0), ("qk_squares", 0), ("qkv_out", 0), ("qkv_out", 1), ("qk_squares", 1), ("qk_rms", 0),
    ("qk_turn", 0), ("qk_norm", 0), ("qkv", 1), ("qk_norm", 1), ("qkv", 2), ("qkv_out", 2), ("qkv", 3),
    ("qk_squares", 2), ("qk_turn", 1), ("qkv_out", 3), ("qk_squares", 3), ("qk_norm", 2), ("qk_norm", 3),
    ("qk_rms", 1),
    ("scores", 0), ("shift", 0), ("exp", 0), ("scores", 1), ("shift", 1), ("qk_turn", 2), ("p_turn", 0),
    ("exp", 1), ("scores", 2), ("shift", 2), ("qk_turn", 3), ("p_turn", 1), ("exp", 2), ("pv", 0),
    ("shift", 3), ("scores", 3), ("exp", 3), ("p_turn", 2), ("o_turn", 0), ("pv", 1), ("p_turn", 3),
    ("o_turn", 1), ("o_turn", 2), ("pv", 2), ("pv", 3), ("o_turn", 3),
    ("on_turn", 0), ("on_turn", 1), ("o_split", 0), ("on_turn", 2), ("on_turn", 3), ("o_split", 1),
    ("res", 0), ("res", 1), ("res_square", 0), ("res_add", 0), ("res_rms", 0), ("res_norm", 0),
    ("res_norm", 1), ("res", 2), ("res_square", 1), ("res_add", 1), ("res", 3), ("res_rms", 1),
    ("res_norm", 2), ("res_norm", 3), ("u_turn", 0), ("u_split", 0), ("u_turn", 1), ("u_turn", 2),
    ("u_turn", 3), ("u_split", 1),
    ("qkv2", 0), ("qkv2_out", 0), ("qkv2", 1), ("qk_turn", 4), ("qkv2_out", 1), ("qkv2", 2), ("qk_turn", 5),
    ("qkv2_out", 2), ("scores", 4), ("exp", 4), ("scores", 5), ("shift", 4), ("qk_turn", 6), ("qkv2_out", 3),
    ("exp", 5), ("shift", 5), ("qkv2", 3), ("p_scale", 4), ("p_sum", 4), ("scores", 6), ("p_turn", 4),
    ("shift", 6), ("exp", 6), ("p_sum", 5), ("p_scale", 5), ("pv", 4), ("qk_turn", 7), ("scores", 7),
    ("p_turn", 5), ("exp", 7), ("shift", 7), ("p_sum", 6), ("p_scale", 6), ("oa_turn", 0), ("pv", 5),
    ("p_turn", 6), ("p_sum", 7), ("oa_turn", 1), ("p_scale", 7), ("p_turn", 7), ("oa_turn", 2), ("pv", 6),
    ("pv", 7), ("oa_turn", 3),
    ("mod", 0), ("m_turn", 0), ("m_turn", 1), ("m_turn", 2), ("m_turn", 3), ("m_out", 0),
]


def ffn_pieces():
    o = []
    for c in range(FC):
        o.append([("up", c)] + ([("gated", c - 1)] if c else []))
        o.append([("gate", c)] + ([("gated_split", c - 1)] if c else []))
    o += [[("gated", FC - 1)], [("gated_split", FC - 1)]]
    for t in range(TILES):
        o.append([("down", t)] + ([("out", t - 1)] if t else []))
    o.append([("out", TILES - 1)])
    return o


FFN_AT = [("qk_norm", 1), ("qkv_out", 2), ("qk_norm", 3), ("qk_rms", 1), ("exp", 0), ("qk_turn", 2),
          ("exp", 1), ("scores", 2), ("qk_turn", 3), ("on_turn", 2), ("res", 0), ("res_rms", 0), ("res", 2),
          ("res_norm", 2), ("u_turn", 0), ("u_split", 0), ("u_split", 0), ("qk_turn", 5), ("p_turn", 4),
          ("shift", 7), ("pv", 6), ("m_turn", 0), ("m_out", 0)]
X_AT = [("qkv2", 0), ("qkv2", 0), ("qkv2", 0), ("qk_turn", 4), ("qk_turn", 4), ("scores", 4), ("exp", 4),
        ("qkv2_out", 3), ("qkv2_out", 3), ("exp", 5), ("exp", 5), ("exp", 5), ("scores", 7), ("oa_turn", 0),
        ("oa_turn", 0), ("oa_turn", 0), ("oa_turn", 0), ("m_out", 0)]


def merged(attention, others):
    out = []
    for s in attention:
        for kind, pieces, at in others:
            for piece, place in zip(pieces, at):
                if place == s:
                    out += [(kind,) + p for p in piece]
        out.append(("attention",) + s)
    return out


PIECES = [("qkv0", 768), ("qkv1", 768), ("w_out", 512), ("q2", 512), ("k2", 512), ("a2", 32),
          ("in0", 1024), ("in1", 1024), ("up0", 1024), ("up1", 1024), ("down0", 1024), ("down1", 1024),
          ("b", 1024)]


def prologue_order(attention):
    out, n = [], 2
    due = {"qkv_out": 1, "scores": 1, "res": 1, "u_turn": 1, "pv": 1}
    for s in attention:
        out.append(s)
        for _ in range(due.get(s[1], 0)):
            if n < len(PIECES):
                out.append(("weights", "piece", n))
                n += 1
                if n == 6:
                    out.append(("weights", "v2", 0))
    while n < len(PIECES):
        out.append(("weights", "piece", n))
        n += 1
    return out


def bass_adaln_attention_ffn(nc, x, condT, w_emb, b_emb, g_norm, w_qkv, gq, gk, w_out, ln1, ln2,
                             wqT, wkT, wv, wo, a_w, b_w, w_inT, w_upT, w_downT,
                             ident_d, heads_d, causal_d, out):
    xv = x.rearrange("(g q t p) d -> g q p t d", q=2, t=2, p=P)
    outv = out.rearrange("(g t p) d -> g t p d", t=TILES, p=P)

    with ExitStack() as ctx:
        def sb(name, shape, dt=F32):
            return ctx.enter_context(nc.sbuf_tensor(name, shape, dt))

        def sem(name):
            return ctx.enter_context(nc.semaphore(name))

        wqkv = [sb(f"wqkv_{s}", [P, KT, 3 * D], F32R) for s in ("hi", "lo")]
        wres = [sb(f"wres_{s}", [P, KT, D], F32R) for s in ("hi", "lo")]
        wqkv2 = [sb(f"wqkv2_{s}", [P, KT, 3 * D + R], F32R) for s in ("hi", "lo")]
        win = [sb(f"win_{s}", [P, KT, FF], F32R) for s in ("hi", "lo")]
        wup = [sb(f"wup_{s}", [P, KT, FF], F32R) for s in ("hi", "lo")]
        wdn = [sb(f"wdn_{s}", [P, FC, D], F32R) for s in ("hi", "lo")]
        b3 = sb("b3", [96, FF], F32R)
        ident = sb("ident", [P, P])
        identb = sb("identb", [P, P], BF16)
        causal = sb("causal", [P, S])
        maskb = sb("maskb", [P, H, S], BF16)
        heads = sb("heads", [P, 8])
        small = sb("small", [P, 16])
        an = sb("an", [P, KT, R])
        gqk = sb("gqk", [P, D])
        scaleT = sb("scaleT", [P, KT, B])
        shiftT = sb("shiftT", [P, KT, B])

        x_sb = [sb(f"x{q}", [P, 2, D]) for q in range(2)]
        tok = sb("tok", [P, TILES, D])
        xm = sb("xm", [P, KT, GROUP])
        ah = sb("ah", [P, KT, GROUP], F32R)
        al = sb("al", [P, KT, GROUP], F32R)
        uh = sb("uh", [P, KT, GROUP], F32R)
        ul = sb("ul", [P, KT, GROUP], F32R)
        sq = sb("sq", [P, 2, 2 * D])
        qk = sb("qk", [P, TILES, 2 * D])
        vs = sb("vs", [P, TILES, D + R])
        qn = sb("qn", [P, 2, D])
        kp = sb("kp", [P, HP, 2, 2, HD])
        qT = sb("qT", [P, 2, D])
        kT = sb("kT", [P, 2, 2 * D])
        z = sb("z", [P, 2, H, S])
        pT = sb("pT", [P, 2, H * S])
        oq = sb("oq", [P, 2, HP, 4 * HD])
        mx = sb("mx", [P, 2, H])
        rsum = sb("rsum", [P, 2, H])
        rinv = sb("rinv", [P, TILES, H])
        ssx = sb("ssx", [P, TILES])
        rx = sb("rx", [P, TILES])
        ssr = sb("ssr", [P, TILES])
        rr = sb("rr", [P, TILES])
        ssq = sb("ssq", [P, TILES, 2 * H])
        rqk = sb("rqk", [P, TILES, 2 * H])
        nw_a = sb("nw_a", [P, 64])
        nw_y = sb("nw_y", [P, 64])
        nw_t = sb("nw_t", [P, 64])
        oa4 = sb("oa4", [P, TILES, 4 * HD])
        oa = sb("oa", [P, TILES, R])
        th16 = sb("th16", [P, TILES, R])
        m16 = sb("m16", [P, TILES, R])
        mt = sb("mt", [P, TILES, 96])
        mT = sb("mT", [96, GROUP], F32R)
        xres = sb("xres", [P, 2, TILES, D])
        gh = sb("gh", [P, FC, GROUP], F32R)
        gl = sb("gl", [P, FC, GROUP], F32R)
        ffn_work = sb("ffn_work", [P, 2048])
        th = ffn_work[:, 0:GROUP]
        g_up = ffn_work[:, GROUP:3 * GROUP].rearrange("p (c n) -> p c n", c=2)
        outb = ffn_work[:, 3 * GROUP:4 * GROUP].rearrange("p (t d) -> p t d", t=2)
        stage = ffn_work[:, 0:2048].rearrange("p (s n) -> p s n", s=2)
        we = xres[:, 1].rearrange("p t d -> p (t d)").rearrange("p (k n) -> p k n", k=KT)
        wvn = xres[:, 0, 0:2, :]
        won = xres[:, 0, 2:4, :]
        cT = xm[:, 0, 0:KT * B].rearrange("p (k n) -> p k n", k=KT)
        mblk = xres[:, 1, 0, :].rearrange("p (k h r) -> p k h r", k=KT, h=8)
        gq_sb = qk[:, 0, 0:D]
        gk_sb = qk[:, 0, D:2 * D]

        A = [ctx.enter_context(nc.psum_tensor(f"attn_bank{i}", [P, 512], F32)) for i in range(4)]
        Fb = [ctx.enter_context(nc.psum_tensor(f"ffn_bank{i}", [P, 512], F32)) for i in range(4)]

        x_loaded = [sem(f"x_loaded{q}") for q in range(2)]
        out_stored = [sem(f"out_stored{t}") for t in range(TILES)]
        emb_loaded = sem("emb_loaded")
        v2_loaded = sem("v2_loaded")
        piece_loaded = [sem(f"piece_loaded{i}") for i in range(2)]
        piece_split = sem("piece_split")
        piece_hi = sem("piece_hi")
        emb_mm, m_mm, v2_mm = sem("emb_mm"), sem("m_mm"), sem("v2_mm")
        prep, mblk_done = sem("prep"), sem("mblk_done")
        v2_hi = sem("v2_hi")
        pads_zeroed = sem("pads_zeroed")
        x_squared, x_rms_done, x_normed, xT_mm = sem("x_squared"), sem("x_rms_done"), sem("x_normed"), sem("xT_mm")
        x_scaled, x_shifted, xh_done, xl_done = sem("x_scaled"), sem("x_shifted"), sem("xh_done"), sem("xl_done")
        qkv_mm, qk_squared, qkv_copied = sem("qkv_mm"), sem("qk_squared"), sem("qkv_copied")
        qk_summed, qk_rms_done, q_scaled, qk_normed = (sem("qk_summed"), sem("qk_rms_done"), sem("q_scaled"),
                                                       sem("qk_normed"))
        qk_turned, scores_mm, maxed, shifted, exped = (sem("qk_turned"), sem("scores_mm"), sem("maxed"),
                                                       sem("shifted"), sem("exped"))
        summed, inverted, scaled, p_turned, pv_mm = (sem("summed"), sem("inverted"), sem("scaled"),
                                                     sem("p_turned"), sem("pv_mm"))
        o_turned, o_normed, oT_mm, oh_done, ol_done = (sem("o_turned"), sem("o_normed"), sem("oT_mm"),
                                                       sem("oh_done"), sem("ol_done"))
        res_mm, res_squared, xres_done, res_rms_done, u_done = (sem("res_mm"), sem("res_squared"),
                                                                sem("xres_done"), sem("res_rms_done"), sem("u_done"))
        uT_mm, uh_done, ul_done, qkv2_mm, qkv2_copied = (sem("uT_mm"), sem("uh_done"), sem("ul_done"),
                                                         sem("qkv2_mm"), sem("qkv2_copied"))
        oa_turned, oa_summed, oa_tanh, m_done, mT_mm, mT_done = (sem("oa_turned"), sem("oa_summed"), sem("oa_tanh"),
                                                      sem("m_done"), sem("mT_mm"), sem("mT_done"))
        newton, m_chain = sem("newton"), sem("m_chain")
        gate_mm, up_mm, tanh_done, half_gated, gated_done = (sem("gate_mm"), sem("up_mm"), sem("tanh_done"),
                                                             sem("half_gated"), sem("gated_done"))
        gh_done, gl_done, down_mm, out_done = sem("gh_done"), sem("gl_done"), sem("down_mm"), sem("out_done")

        credit = [gated_done, gl_done, down_mm, out_done, *out_stored]

        def wait(eng, s, per_group, g, n):
            if any(s is c for c in credit):
                n += per_group
            if isinstance(g, int):
                if g * per_group + n > 0:
                    eng.wait_ge(s, g * per_group + n)
            else:
                eng.wait_ge(s, g * per_group + n)

        attention = ATTENTION
        x_pieces = [[p] for p in x_order()]
        steady = merged(attention, [("ffn", ffn_pieces(), FFN_AT), ("x", x_pieces, X_AT)])
        first = prologue_order(merged(attention, [("x", x_pieces, X_AT)]))

        def run(eng, do_attention, do_ffn, do_weights, loop_starts=lambda g: None):
            for name, i in x_order():
                do_attention(name, 0, i)
            for kind, name, i in first:
                if kind == "weights":
                    do_weights(name, i)
                else:
                    do_attention(name, 1 if kind == "x" else 0, i)
            with eng.Fori(1, GROUPS - 1) as g:
                loop_starts(g)
                for kind, name, i in steady:
                    if kind == "ffn":
                        do_ffn(name, g - 1, i)
                    else:
                        do_attention(name, g + 1 if kind == "x" else g, i)
            loop_starts(None)
            for kind, name, i in steady:
                if kind == "ffn":
                    do_ffn(name, GROUPS - 2, i)
                elif kind == "attention":
                    do_attention(name, GROUPS - 1, i)
            for piece in ffn_pieces():
                for name, i in piece:
                    do_ffn(name, GROUPS - 1, i)

        piece_names = [n for n, _ in PIECES]

        def piece_parts(n):
            name = piece_names[n]
            st = stage[:, n % 2, 0:PIECES[n][1]]
            if name[:3] == "qkv":
                k = int(name[3])
                return [(st, wqkv[0][:, k, :], wqkv[1][:, k, :], 1.0)]
            if name == "w_out":
                st = st.rearrange("p (k n) -> p k n", k=KT)
                return [(st, wres[0][:, :, :], wres[1][:, :, :], 1.0)]
            if name in ("q2", "k2", "a2"):
                w = R if name == "a2" else D
                lo = {"q2": 0, "k2": D, "a2": 3 * D}[name]
                first_col = {"q2": 12, "k2": 8, "a2": 10}[name]
                st = st.rearrange("p (k n) -> p k n", k=KT)
                return [(st[:, k, :], wqkv2[0][:, k, lo:lo + w], wqkv2[1][:, k, lo:lo + w],
                         small[:, first_col + k:first_col + k + 1]) for k in range(KT)]
            if name[:2] in ("in", "up"):
                k = int(name[2])
                w = win if name[:2] == "in" else wup
                return [(st, w[0][:, k, :], w[1][:, k, :], small[:, 10 + k:11 + k])]
            if name[:4] == "down":
                k = int(name[4])
                st = st.rearrange("p (k n) -> p k n", k=FC // 2)
                sl = slice(k * FC // 2, (k + 1) * FC // 2)
                return [(st, wdn[0][:, sl, :], wdn[1][:, sl, :], 0.5)]
            return []

        def half(buf, q):
            return buf[:, :, q * 2 * P:(q + 1) * 2 * P]

        def by_k(bank):
            return bank[:, :].rearrange("p (k n) -> p k n", k=KT)

        def by_seq(ap):
            return ap.rearrange("p k (b s) -> p k b s", s=S)

        def padded(src):
            whole = kp[:, :, :, :, :].rearrange("p a b c d -> p a (b c d)")
            dst = bass.AP(whole.tensor, whole.offset, [whole.ap[0], [4 * HD, HP], [3 * HD, 2], [1, HD]])
            return dst, src.rearrange("p (a b d) -> p a b d", a=HP, b=2)

        def own_head(src):
            return bass.AP(src.tensor, src.offset, [src.ap[0], [4 * HD, HP], [3 * HD, 2], [1, HD]])

        block = ctx.enter_context(nc.Block())

        @block.sync
        def _(sp):
            def load_x(g, q):
                wait(sp, xres_done, 2, g, q - 1)
                src = xv[bass.ds(g, 1), q].rearrange("g p t d -> p (g t) d")
                sp.dma_start(x_sb[q][:, :, :], src).then_inc(x_loaded[q], 16)

            def load_piece(n):
                if n >= 2:
                    sp.wait_ge(piece_split, n - 1)
                name = piece_names[n]
                to = piece_loaded[n % 2]
                dst = stage[:, n % 2, 0:PIECES[n][1]]
                if name == "b":
                    for j in range(3):
                        sp.dma_start(stage[32 * j:32 * j + R, n % 2, :], b_w).then_inc(to, 16)
                    return
                if name[:3] == "qkv":
                    k = int(name[3])
                    src = w_qkv[k * P:(k + 1) * P, :]
                elif name[:2] in ("in", "up"):
                    k = int(name[2])
                    src = (w_inT if name[:2] == "in" else w_upT)[k * P:(k + 1) * P, :]
                elif name[:4] == "down":
                    k = int(name[4])
                    src = w_downT[k * FF // 2:(k + 1) * FF // 2, :].rearrange("(k p) n -> p k n", p=P)
                    dst = dst.rearrange("p (k n) -> p k n", k=FC // 2)
                else:
                    w = {"w_out": w_out, "q2": wqT, "k2": wkT, "a2": a_w}[name]
                    src = w.rearrange("(k p) n -> p k n", p=P)
                    dst = dst.rearrange("p (k n) -> p k n", k=KT)
                sp.dma_start(dst, src).then_inc(to, 16)

            load_x(0, 0)
            load_x(0, 1)
            sp.dma_start(ident[:, :], ident_d).then_inc(emb_loaded, 16)
            sp.dma_start(we, w_emb.rearrange("(k p) n -> p k n", p=P)).then_inc(emb_loaded, 16)
            sp.dma_start(cT, condT.rearrange("(k p) n -> p k n", p=P)).then_inc(emb_loaded, 16)
            for col, v, n in ((0, b_emb, 4), (6, g_norm, 2), (8, ln1, 2), (10, ln2, 2)):
                with nc.allow_non_contiguous_dma(reason="vectors of features onto partitions"):
                    sp.dma_start(small[:, col:col + n], v.rearrange("(k p) -> p k", p=P)).then_inc(emb_loaded, 16)
            sp.dma_start(gq_sb, gq).then_inc(emb_loaded, 16)
            sp.dma_start(gk_sb, gk).then_inc(emb_loaded, 16)
            sp.dma_start(causal[:, :], causal_d).then_inc(emb_loaded, 16)
            load_piece(0)
            load_piece(1)
            sp.dma_start(heads[:, :], heads_d).then_inc(v2_loaded, 16)
            sp.dma_start(won, wo.rearrange("(k p) n -> p k n", p=P)).then_inc(v2_loaded, 16)
            sp.dma_start(wvn, wv.rearrange("(k p) n -> p k n", p=P)).then_inc(v2_loaded, 16)
            sp.dma_start(an[:, :, :], a_w.rearrange("(k p) n -> p k n", p=P)).then_inc(v2_loaded, 16)
            for n in range(2, len(PIECES)):
                load_piece(n)
            load_x(1, 0)
            load_x(1, 1)

            def store(g, t):
                wait(sp, out_done, TILES, g, t + 1)
                dst = outv[bass.ds(g, 1), t].rearrange("g p d -> p (g d)")
                sp.dma_start(dst, outb[:, t % 2, :]).then_inc(out_stored[t], 16)

            with sp.Fori(1, GROUPS - 1) as g:
                load_x(g + 1, 0)
                load_x(g + 1, 1)
                for t in range(TILES):
                    store(g - 1, t)
            for g in (GROUPS - 2, GROUPS - 1):
                for t in range(TILES):
                    store(g, t)
            for t in range(TILES):
                sp.wait_ge(out_stored[t], 16 * (GROUPS + 1))

        @block.tensor
        def _(pe):
            def three_passes(dst, stat, mov, first_mm, last_mm):
                for j, (a, b) in enumerate(((0, 0), (0, 1), (1, 0))):
                    mm = pe.matmul(dst, stat[a], mov[b], start=first_mm and j == 0, stop=last_mm and j == 2)
                return mm

            def token_major(dsts, stat_hi, stat_lo, w, cols, t):
                for k in range(KT):
                    for j, (a, b) in enumerate(((stat_hi, 0), (stat_hi, 1), (stat_lo, 0))):
                        for dst, (c0, c1) in zip(dsts, cols):
                            mm = pe.matmul(dst, a[:, k, t * P:(t + 1) * P], w[b][:, k, c0:c1],
                                           start=(k == 0 and j == 0), stop=(k == KT - 1 and j == 2))
                return mm

            def turn(bank, t):
                for k in range(KT):
                    c = (k * 2 + t % 2) * P
                    mm = pe.transpose(bank[:, c:c + P], tok[:, t, k * P:(k + 1) * P], ident[:, :])
                return mm

            def do_attention(name, g, i):
                t = i
                if name == "x_turn":
                    wait(pe, x_normed, TILES, g, t + 1)
                    if t == 0:
                        wait(pe, gated_done, FC, g, -FC - 1)
                    turn(Fb[t // 2], t).then_inc(xT_mm, 1)
                elif name == "qkv":
                    if t % 2 == 0:
                        wait(pe, xl_done, 2, g, t // 2 + 1)
                    if t == 0:
                        wait(pe, mT_done, 1, g, 0)
                        wait(pe, oa_turned, TILES, g, 0)
                    elif t == 1:
                        wait(pe, oa_turned, TILES, g, 0)
                    else:
                        wait(pe, qkv_copied, TILES, g, t - 1)
                    if isinstance(g, int) and t == 0:
                        pe.wait_ge(piece_split, 2)
                    pair = 2 * (t % 2)
                    token_major([A[pair][:, :], A[pair + 1][:, 0:D]], ah, al, wqkv, [(0, 512), (512, 768)],
                                t).then_inc(qkv_mm, 1)
                elif name == "scores":
                    n, second = i, i >= TILES
                    t = n % TILES
                    wait(pe, qk_turned, 2 * TILES, g, n + 1)
                    pair_reader = 2 if t < 2 else 3
                    wait(pe, qkv2_copied if second else qkv_copied, TILES, g, pair_reader + 1)
                    if second:
                        pe.matmul(A[t][:, :], identb[:, :], maskb[:, :, :].rearrange("p h s -> p (h s)"),
                                  start=True, stop=False, skip_group_check=True)
                    for hp in range(HP):
                        for b in range(4):
                            rows = slice(32 * b, 32 * b + 32)
                            wide = 32 * (not second and hp + b == 0)
                            dst = slice(32 * b, 32 * b + 32 + wide)
                            mm = pe.matmul(A[t][dst, 64 * hp:64 * hp + 64], qT[rows, n % 2, 32 * hp:32 * hp + 32 + wide],
                                           kT[rows, n % 2, 64 * hp:64 * hp + 64], start=not second, stop=True,
                                           skip_group_check=True)
                    mm.then_inc(scores_mm, 1)
                elif name == "pv":
                    n, second = i, i >= TILES
                    t = n % TILES
                    wait(pe, p_turned, 2 * TILES, g, n + 1)
                    for hp in range(HP):
                        for b in range(4):
                            rows = slice(32 * b, 32 * b + 32)
                            wide = 32 * (hp + b == 0)
                            out_rows = slice(32 * b, 32 * b + 32 + wide)
                            dst = A[t][out_rows, 0:64] if second else A[t][out_rows, 64 * hp:64 * hp + 64]
                            mm = pe.matmul(dst, vs[rows, t, 32 * hp:32 * hp + 32 + wide],
                                           pT[rows, n % 2, 64 * hp:64 * hp + 64],
                                           start=(not second or hp == 0), stop=(not second or hp == HP - 1),
                                           skip_group_check=True)
                    mm.then_inc(pv_mm, 1)
                elif name == "on_turn":
                    wait(pe, o_normed, TILES, g, t + 1)
                    if t % 2 == 0:
                        wait(pe, o_turned, TILES, g, t // 2 + 1)
                    turn(A[t // 2], t).then_inc(oT_mm, 1)
                elif name == "res":
                    if t % 2 == 0:
                        wait(pe, ol_done, 2, g, t // 2 + 1)
                    if t == 0:
                        wait(pe, o_turned, TILES, g, TILES)
                        if isinstance(g, int):
                            pe.wait_ge(piece_split, 3)
                    dst = A[2 + t // 2][:, (t % 2) * D:(t % 2 + 1) * D]
                    token_major([dst], ah, al, wres, [(0, D)], t).then_inc(res_mm, 1)
                elif name == "u_turn":
                    wait(pe, u_done, TILES, g, t + 1)
                    if t % 2 == 0:
                        wait(pe, ol_done, 2, g, t // 2 + 1)
                    turn(A[t // 2], t).then_inc(uT_mm, 1)
                elif name == "qkv2":
                    if t % 2 == 0:
                        wait(pe, ul_done, 2, g, t // 2 + 1)
                    if t == 0:
                        wait(pe, ul_done, 2, g, 2)
                        if isinstance(g, int):
                            pe.wait_ge(piece_split, 6)
                            pe.wait_ge(v2_hi, 2)
                    elif t == 1:
                        wait(pe, u_done, TILES, g, TILES)
                    else:
                        wait(pe, qkv2_copied, TILES, g, t - 1)
                    pair = 2 * (t % 2)
                    token_major([A[pair][:, :], A[pair + 1][:, 0:D + R]], uh, ul, wqkv2,
                                [(0, 512), (512, 768 + R)], t).then_inc(qkv2_mm, 1)
                elif name == "m_turn":
                    if t == 0:
                        wait(pe, m_done, 1, g, 1)
                        wait(pe, oa_turned, TILES, g, TILES)
                    pe.transpose(A[0][0:96, t * P:(t + 1) * P], mt[:, t, :], ident[:, :]).then_inc(mT_mm, 1)

            def do_ffn(name, g, i):
                c = i
                if name in ("gate", "up"):
                    bank = Fb[2 * (c % 2) + (name == "up")]
                    w = win if name == "gate" else wup
                    if c >= 2:
                        wait(pe, gated_done, FC, g, c - 1)
                    elif name == "up" and c == 0:
                        wait(pe, x_scaled, 2, g, 4 if not (isinstance(g, int) and g == GROUPS - 1) else 2)
                    elif name == "up":
                        wait(pe, out_done, TILES, g, 0)
                    fs = slice(c * P, (c + 1) * P)
                    for k in range(KT):
                        mm = three_passes(bank[:, :], (w[0][:, k, fs], w[1][:, k, fs]), (uh[:, k, :], ul[:, k, :]),
                                          k == 0, name == "up" and k == KT - 1)
                    if name == "gate":
                        if c == 0:
                            wait(pe, mT_done, 1, g, 1)
                        mm = pe.matmul(bank[:, :], b3[:, c * P:(c + 1) * P], mT[:, :], start=False, stop=True)
                        mm.then_inc(gate_mm, 1)
                    else:
                        mm.then_inc(up_mm, 1)
                elif name == "down":
                    t = i
                    if t == 0:
                        wait(pe, gl_done, FC, g, FC)
                    elif t >= 2:
                        wait(pe, out_done, TILES, g, t - 1)
                    for c in range(FC):
                        mm = three_passes(Fb[2 + t % 2][:, 0:D], (gh[:, c, t * P:(t + 1) * P], gl[:, c, t * P:(t + 1) * P]),
                                          (wdn[0][:, c, :], wdn[1][:, c, :]), c == 0, c == FC - 1)
                    mm.then_inc(down_mm, 1)

            def do_weights(name, n):
                if name == "piece" and piece_names[n] == "w_out":
                    pe.wait_ge(v2_loaded, 64)
                    pe.wait_ge(pads_zeroed, 3)
                    for m in range(KT):
                        for k in range(KT):
                            mm = pe.matmul(Fb[3][:, m * R:(m + 1) * R], won[:, k, m * P:(m + 1) * P], an[:, k, :],
                                           start=(k == 0), stop=(k == KT - 1))
                    mm.then_inc(m_mm, 1)
                elif name == "v2":
                    pe.wait_ge(mblk_done, 1)
                    for f in range(KT):
                        for m in range(KT):
                            mm = pe.matmul(Fb[2][:, f * D + m * P:f * D + (m + 1) * P],
                                           wvn[:, m, f * P:(f + 1) * P],
                                           mblk[:, m, :, :].rearrange("p h r -> p (h r)"), start=True, stop=True)
                    mm.then_inc(v2_mm, 1)

            pe.wait_ge(emb_loaded, 16 * 10)
            for m in range(4):
                for k in range(KT):
                    mm = pe.matmul(Fb[3][:, m * B:(m + 1) * B], we[:, k, m * P:(m + 1) * P], cT[:, k, :],
                                   start=(k == 0), stop=(k == KT - 1))
                if m == 0:
                    mm.then_inc(down_mm, TILES)
            mm.then_inc(emb_mm, 1)
            run(pe, do_attention, do_ffn, do_weights)

        @block.scalar
        def _(act):
            def do_attention(name, g, i):
                t = i
                if name == "x_square":
                    wait(act, x_loaded[t // 2], 16, g, 16)
                    wait(act, uT_mm, TILES, g, t - 3)
                    act.activation(tok[:, t, :], x_sb[t // 2][:, t % 2, :], ACT.Square,
                                   accum_out=ssx[:, t:t + 1]).then_inc(x_squared, 1)
                elif name == "x_norm":
                    wait(act, x_rms_done, 2, g, t // 2 + 1)
                    act.activation(tok[:, t, :], x_sb[t // 2][:, t % 2, :], ACT.Copy,
                                   scale=rx[:, t:t + 1]).then_inc(x_normed, 1)
                elif name == "x_split":
                    wait(act, x_shifted, 2, g, i + 1)
                    wait(act, res_mm, TILES, g, 0)
                    act.activation(half(ah, i), half(xm, i), ACT.Copy).then_inc(xh_done, 1)
                elif name == "qkv_out":
                    pair = 2 * (t % 2)
                    wait(act, qkv_mm, TILES, g, t + 1)
                    wait(act, qk_summed, TILES, g, t - 1)
                    act.activation(sq[:, t % 2, :], A[pair][:, :], ACT.Square).then_inc(qk_squared, 1)
                    wait(act, qk_normed, TILES, g, t - 3)
                    act.activation(qk[:, t, :], A[pair][:, :], ACT.Copy)
                    wait(act, pv_mm, 2 * TILES, g, t - 3)
                    act.activation(vs[:, t, 0:D], A[pair + 1][:, 0:D], ACT.Copy).then_inc(qkv_copied, 1)
                elif name == "exp":
                    wait(act, shifted, 2 * TILES, g, i + 1)
                    act.activation(z[:, i % 2], z[:, i % 2], ACT.Exp).then_inc(exped, 1)
                elif name == "o_split":
                    wait(act, oT_mm, TILES, g, 2 * i + 2)
                    wait(act, qkv_mm, TILES, g, TILES)
                    act.activation(half(ah, i), by_k(A[i]), ACT.Copy).then_inc(oh_done, 1)
                elif name == "res_square":
                    for t in (2 * i, 2 * i + 1):
                        wait(act, res_mm, TILES, g, 2 * i + 2)
                        act.activation(tok[:, t, :], A[2 + i][:, (t % 2) * D:(t % 2 + 1) * D], ACT.Square,
                                       accum_out=ssr[:, t:t + 1]).then_inc(res_squared, 1)
                elif name == "res_norm":
                    wait(act, res_rms_done, 2, g, t // 2 + 1)
                    act.activation(tok[:, t, :], A[2 + t // 2][:, (t % 2) * D:(t % 2 + 1) * D], ACT.Copy,
                                   scale=rr[:, t:t + 1]).then_inc(u_done, 1)
                elif name == "u_split":
                    wait(act, uT_mm, TILES, g, 2 * i + 2)
                    wait(act, gate_mm, FC, g, 0)
                    act.activation(half(uh, i), by_k(A[i]), ACT.Copy).then_inc(uh_done, 1)
                elif name == "qkv2_out":
                    n = TILES + t
                    pair = 2 * (t % 2)
                    wait(act, qkv2_mm, TILES, g, t + 1)
                    wait(act, qk_turned, 2 * TILES, g, n - 1)
                    act.activation(qn[:, n % 2, :], A[pair][:, 0:D], ACT.Copy)
                    wait(act, qk_turned, 2 * TILES, g, n)
                    kdst, ksrc = padded(A[pair][:, D:2 * D])
                    act.activation(kdst, ksrc, ACT.Copy)
                    wait(act, pv_mm, 2 * TILES, g, t + 1)
                    act.activation(vs[:, t, :], A[pair + 1][:, 0:D + R], ACT.Copy).then_inc(qkv2_copied, 1)
                elif name == "mod":
                    wait(act, oa_summed, TILES, g, TILES)
                    act.activation(th16[:, :, :], oa[:, :, :], ACT.Tanh).then_inc(oa_tanh, 1)
                elif name == "m_out":
                    wait(act, mT_mm, TILES, g, TILES)
                    wait(act, gate_mm, FC, g, 0)
                    act.activation(mT[:, :], A[0][0:96, :], ACT.Copy).then_inc(mT_done, 1)

            def do_ffn(name, g, i):
                c = i
                if name == "gate":
                    wait(act, gate_mm, FC, g, c + 1)
                    wait(act, gated_done, FC, g, c)
                    act.activation(th, Fb[2 * (c % 2)][:, :], ACT.Tanh, scale=0.5).then_inc(tanh_done, 1)
                elif name == "gated_split":
                    wait(act, gated_done, FC, g, c + 1)
                    wait(act, down_mm, TILES, g, 0)
                    act.activation(gh[:, c, :], g_up[:, c % 2, :], ACT.Copy).then_inc(gh_done, 1)

            def do_weights(name, n):
                if name == "v2":
                    act.wait_ge(v2_mm, 1)
                    for k in range(KT):
                        hi = act.activation(wqkv2[0][:, k, 512:768], Fb[2][:, k * D:(k + 1) * D], ACT.Copy,
                                            scale=small[:, 8 + k:9 + k])
                    hi.then_inc(v2_hi, 1)
                    return
                if piece_names[n] == "b":
                    return
                act.wait_ge(piece_loaded[n % 2], 16 * (n // 2 + 1))
                if piece_names[n] == "w_out":
                    act.wait_ge(prep, 3)
                for st, hi_ap, _, scale in piece_parts(n):
                    hi = act.activation(hi_ap, st, ACT.Copy, scale=scale)
                hi.then_inc(piece_hi, 1)

            do_weights("piece", 0)
            do_weights("piece", 1)
            act.wait_ge(prep, 2)
            run(act, do_attention, do_ffn, do_weights)

        @block.vector
        def _(dve):
            count = {"steps": 0, "ahead": 0, "per_pass": 0, "passes": 0}

            def loop_starts(g):
                if g is None:
                    count.update(steps=count["ahead"] + (GROUPS - 2) * count["per_pass"], ahead=0, passes=0)
                else:
                    count.update(ahead=count["steps"], per_pass=count["steps"] - count["adaln"], steps=0,
                                 passes=g - 1)

            def rsqrt(dst, src, n, g, signal):
                w = dst.shape[-1] if len(dst.shape) == 2 else dst.shape[-1] * dst.shape[-2]
                a, y, u = nw_a[:, 0:w], nw_y[:, 0:w], nw_t[:, 0:w]
                base = count["ahead"] + count["passes"] * count["per_pass"]

                def then(ins):
                    count["steps"] += 1
                    ins.then_inc(newton, 1)
                    dve.wait_ge(newton, base + count["steps"])

                then(dve.tensor_scalar(a, src, 1.0 / n, EPS, ALU.mult, ALU.add))
                then(dve.tensor_scalar(y.bitcast(I32), a.bitcast(I32), 1, None, ALU.arith_shift_right))
                then(dve.tensor_scalar(y.bitcast(I32), y.bitcast(I32), -1, RSQRT_GUESS, ALU.mult, ALU.add))
                for s in range(NEWTON_STEPS):
                    then(dve.scalar_tensor_tensor(out=u, in0=y, scalar=-0.5, in1=y, op0=ALU.mult, op1=ALU.mult))
                    then(dve.tensor_tensor(u, u, a, ALU.mult))
                    if s < NEWTON_STEPS - 1:
                        then(dve.scalar_tensor_tensor(out=y, in0=u, scalar=1.5, in1=y, op0=ALU.add, op1=ALU.mult))
                dve.scalar_tensor_tensor(out=dst, in0=u, scalar=1.5, in1=y, op0=ALU.add,
                                         op1=ALU.mult).then_inc(signal, 1)

            def do_attention(name, g, i):
                t = i
                if name == "x_rms":
                    wait(dve, x_squared, TILES, g, 2 * i + 2)
                    rsqrt(rx[:, 2 * i:2 * i + 2], ssx[:, 2 * i:2 * i + 2], D, g, x_rms_done)
                elif name == "x_modulate":
                    wait(dve, xT_mm, TILES, g, 2 * i + 2)
                    wait(dve, xh_done, 2, g, i - 1)
                    sc = scaleT[:, :, bass.ds(g * SEQS + i * SEQS // 2, SEQS // 2)]
                    dve.tensor_tensor(by_seq(half(xm, i)), by_seq(by_k(Fb[i])),
                                      sc.unsqueeze(3).to_broadcast([P, KT, SEQS // 2, S]),
                                      ALU.mult).then_inc(x_scaled, 1)
                elif name == "x_split":
                    if isinstance(g, int) and g == 0:
                        count["adaln"] = count["steps"]
                    wait(dve, xh_done, 2, g, i + 1)
                    dve.tensor_tensor(half(al, i), half(xm, i), half(ah, i).bitcast(F32),
                                      ALU.subtract).then_inc(xl_done, 1)
                elif name == "qk_squares":
                    wait(dve, qk_squared, TILES, g, t + 1)
                    wait(dve, qk_rms_done, 2, g, t // 2 - 1)
                    dve.tensor_reduce(ssq[:, t, :], sq[:, t % 2, :].rearrange("p (h d) -> p h d", d=HD), AX_X,
                                      ALU.add).then_inc(qk_summed, 1)
                elif name == "qk_rms":
                    wait(dve, qk_summed, TILES, g, 2 * i + 2)
                    wait(dve, qk_normed, TILES, g, 2 * i - 2)
                    rsqrt(rqk[:, 2 * i:2 * i + 2, :].rearrange("p t h -> p (t h)"),
                          ssq[:, 2 * i:2 * i + 2, :].rearrange("p t h -> p (t h)"), HD, g, qk_rms_done)
                elif name == "qk_turn":
                    n = i
                    if n < TILES:
                        wait(dve, qk_normed, TILES, g, n + 1)
                    else:
                        wait(dve, qkv2_copied, TILES, g, n - TILES + 1)
                    wait(dve, scores_mm, 2 * TILES, g, n - 1)
                    dve.transpose(qT[:, n % 2, :], qn[:, n % 2, :])
                    dve.transpose(kT[:, n % 2, :],
                                  kp[:, :, :, :, :].rearrange("p a b c d -> p (a b c d)")).then_inc(qk_turned, 1)
                elif name == "shift":
                    n, t = i, i % TILES
                    wait(dve, scores_mm, 2 * TILES, g, n + 1)
                    sc = A[t][:, :].rearrange("p (h s) -> p h s", s=S)
                    dve.tensor_reduce(mx[:, n % 2, :], sc, AX_X, ALU.max).then_inc(maxed, 1)
                    wait(dve, maxed, 2 * TILES, g, n + 1)
                    wait(dve, p_turned, 2 * TILES, g, n - 1)
                    dve.tensor_tensor(z[:, n % 2], sc, mx[:, n % 2, :].unsqueeze(2).to_broadcast([P, H, S]),
                                      ALU.subtract).then_inc(shifted, 1)
                elif name in ("p_sum", "p_turn"):
                    n, t = i, i % TILES
                    if name == "p_sum" or n < TILES:
                        wait(dve, exped, 2 * TILES, g, n + 1)
                        wait(dve, inverted, 2 * TILES, g, n)
                        dve.tensor_reduce(rsum[:, n % 2, :], z[:, n % 2], AX_X, ALU.add).then_inc(summed, 1)
                        wait(dve, summed, 2 * TILES, g, n + 1)
                        wait(dve, o_normed if n >= TILES else scaled, TILES, g, t + 1 if n >= TILES else t - 3)
                        dve.reciprocal(rinv[:, t, :], rsum[:, n % 2, :]).then_inc(inverted, 1)
                    if name == "p_turn":
                        if n >= TILES:
                            wait(dve, scaled, TILES, g, t + 1)
                        wait(dve, pv_mm, 2 * TILES, g, n - 1)
                        dve.transpose(pT[:, n % 2, :],
                                      z[:, n % 2].rearrange("p h s -> p (h s)")).then_inc(p_turned, 1)
                elif name == "o_turn":
                    wait(dve, pv_mm, 2 * TILES, g, t + 1)
                    wait(dve, o_normed, TILES, g, t - 1)
                    dve.transpose(oq[:, t % 2].rearrange("p a b -> p (a b)"), A[t][:, :]).then_inc(o_turned, 1)
                elif name == "o_split":
                    wait(dve, oh_done, 2, g, i + 1)
                    dve.tensor_tensor(half(al, i), by_k(A[i]), half(ah, i).bitcast(F32),
                                      ALU.subtract).then_inc(ol_done, 1)
                elif name == "res_add":
                    wait(dve, res_squared, TILES, g, 2 * i + 2)
                    wait(dve, out_done, TILES, g, -TILES)
                    dst = xres[:, bass.ds(g % 2, 1), 2 * i:2 * i + 2, :].rearrange("p g t d -> p (g t) d")
                    dve.tensor_tensor(dst, A[2 + i][:, :].rearrange("p (t d) -> p t d", t=2), x_sb[i][:, :, :],
                                      ALU.add).then_inc(xres_done, 1)
                elif name == "res_rms":
                    rsqrt(rr[:, 2 * i:2 * i + 2], ssr[:, 2 * i:2 * i + 2], D, g, res_rms_done)
                elif name == "u_split":
                    wait(dve, uh_done, 2, g, i + 1)
                    dve.tensor_tensor(half(ul, i), by_k(A[i]), half(uh, i).bitcast(F32),
                                      ALU.subtract).then_inc(ul_done, 1)
                elif name == "oa_turn":
                    wait(dve, pv_mm, 2 * TILES, g, TILES + t + 1)
                    dve.transpose(oa4[:, t, :], A[t][:, 0:64]).then_inc(oa_turned, 1)
                    wait(dve, oa_turned, TILES, g, t + 1)
                    ins = dve.tensor_tensor(oa[:, t, :], oa4[:, t, 0:HD], oa4[:, t, 3 * HD:4 * HD], ALU.add)
                    ins.then_inc(oa_summed, 1)
                elif name == "mod":
                    wait(dve, oa_tanh, 1, g, 1)
                    wait(dve, mT_mm, TILES, g, 0)
                    dve.scalar_tensor_tensor(out=m16[:, :, :], in0=th16[:, :, :], scalar=0.1,
                                             in1=vs[:, :, D:D + R], op0=ALU.mult, op1=ALU.mult).then_inc(m_chain, 1)
                    wait(dve, m_chain, 2, g, 1)
                    dve.tensor_copy(mt[:, :, 0:R].bitcast(F32R), m16[:, :, :])
                    dve.tensor_copy(mt[:, :, 64:64 + R].bitcast(F32R), m16[:, :, :]).then_inc(m_chain, 1)
                    wait(dve, m_chain, 2, g, 2)
                    dve.tensor_tensor(mt[:, :, 32:32 + R], m16[:, :, :], mt[:, :, 64:64 + R],
                                      ALU.subtract).then_inc(m_done, 1)

            def do_ffn(name, g, i):
                c = i
                if name == "gated":
                    wait(dve, tanh_done, FC, g, c + 1)
                    dve.scalar_tensor_tensor(out=th, in0=th, scalar=1.0, in1=Fb[2 * (c % 2)][:, :], op0=ALU.add,
                                             op1=ALU.mult).then_inc(half_gated, 1)
                    wait(dve, half_gated, FC, g, c + 1)
                    wait(dve, up_mm, FC, g, c + 1)
                    wait(dve, gl_done, FC, g, max(c - 1, 0))
                    dve.tensor_tensor(g_up[:, c % 2, :], th, Fb[2 * (c % 2) + 1][:, :],
                                      ALU.mult).then_inc(gated_done, 1)
                elif name == "out":
                    t = i
                    wait(dve, down_mm, TILES, g, t + 1)
                    if t < 2:
                        wait(dve, out_stored[t + 2], 16, g, 0)
                    else:
                        wait(dve, out_stored[t - 2], 16, g, 16)
                    wait(dve, xres_done, 2, g, 2)
                    src = xres[:, bass.ds(g % 2, 1), t, :].rearrange("p g d -> p (g d)")
                    dve.tensor_tensor(outb[:, t % 2, :], Fb[2 + t % 2][:, 0:D], src, ALU.add).then_inc(out_done, 1)

            def do_weights(name, n):
                if name == "v2":
                    dve.wait_ge(v2_hi, 1)
                    for k in range(KT):
                        lo = dve.scalar_tensor_tensor(out=wqkv2[1][:, k, 512:768], in0=Fb[2][:, k * D:(k + 1) * D],
                                                      scalar=small[:, 8 + k:9 + k],
                                                      in1=wqkv2[0][:, k, 512:768].bitcast(F32),
                                                      op0=ALU.mult, op1=ALU.subtract)
                    lo.then_inc(v2_hi, 1)
                    return
                name = piece_names[n]
                if name == "b":
                    dve.wait_ge(piece_loaded[n % 2], 16 * (n // 2 + 3))
                    dve.wait_ge(pads_zeroed, 2)
                    for j in range(3):
                        rows = slice(32 * j, 32 * j + R)
                        ins = dve.tensor_copy(b3[rows, :], stage[rows, n % 2, :])
                    ins.then_inc(prep, 1)
                    dve.wait_ge(prep, 4)
                    dve.tensor_tensor(b3[64:64 + R, :], stage[64:64 + R, n % 2, :], b3[64:64 + R, :].bitcast(F32),
                                      ALU.subtract).then_inc(piece_split, 1)
                    return
                if name == "w_out":
                    dve.wait_ge(m_mm, 1)
                    for m in range(KT):
                        mb = dve.tensor_tensor(mblk[:, m], Fb[3][:, m * R:(m + 1) * R].unsqueeze(1).to_broadcast([P, 8, R]),
                                               heads[:, :].unsqueeze(2).to_broadcast([P, 8, R]), ALU.mult)
                    mb.then_inc(mblk_done, 1)
                    dve.wait_ge(piece_loaded[n % 2], 16 * (n // 2 + 1))
                    for k in range(KT):
                        seg = stage[:, n % 2, k * D + k * P:k * D + (k + 1) * P]
                        ins = dve.tensor_tensor(seg, seg, ident[:, :], ALU.add)
                    ins.then_inc(prep, 1)
                dve.wait_ge(piece_hi, n + 1)
                parts = piece_parts(n)
                for j, (st, hi_ap, lo_ap, scale) in enumerate(parts):
                    ins = dve.scalar_tensor_tensor(out=lo_ap, in0=st, scalar=scale, in1=hi_ap.bitcast(F32),
                                                   op0=ALU.mult, op1=ALU.subtract)
                ins.then_inc(piece_split, 1)

            dve.memset(kp[:, :, :, :, :], 0.0).then_inc(gated_done, FC)
            for t in range(TILES):
                dve.memset(mx[:, 0, t:t + 1], 0.0).then_inc(out_stored[t], 16)
            dve.memset(mx[:, 0, TILES:TILES + 1], 0.0).then_inc(out_done, TILES)
            dve.memset(mt[:, :, :], 0.0).then_inc(pads_zeroed, 1)
            dve.memset(b3[:, :].bitcast(F32), 0.0).then_inc(pads_zeroed, 1)
            dve.wait_ge(emb_loaded, 16 * 10)
            dve.tensor_scalar(small[:, 12:14], small[:, 8:10], 0.25, None, ALU.mult)
            dve.tensor_scalar(small[:, 4:6], small[:, 0:2], 1.0, None, ALU.add).then_inc(prep, 1)
            dve.tensor_copy(identb[:, :], ident[:, :])
            dve.tensor_copy(maskb[:, :, :], causal[:, :].unsqueeze(1).to_broadcast([P, H, S]))
            dve.scalar_tensor_tensor(out=gqk[:, :], in0=gq_sb, scalar=float(HD) ** -0.5, in1=gk_sb,
                                     op0=ALU.mult, op1=ALU.mult).then_inc(prep, 1)
            dve.wait_ge(emb_mm, 1)
            dve.wait_ge(prep, 2)
            for k in range(KT):
                dve.tensor_scalar(scaleT[:, k, :], Fb[3][:, k * B:(k + 1) * B], small[:, 4 + k:5 + k],
                                  small[:, 6 + k:7 + k], ALU.add, ALU.mult)
                ins = dve.tensor_scalar(shiftT[:, k, :], Fb[3][:, (2 + k) * B:(3 + k) * B], small[:, 2 + k:3 + k],
                                        None, ALU.add)
            ins.then_inc(pads_zeroed, 1)
            do_weights("piece", 0)
            do_weights("piece", 1)
            run(dve, do_attention, do_ffn, do_weights, loop_starts)

        @block.gpsimd
        def _(pool):
            def do_attention(name, g, i):
                t = i
                if name == "x_modulate":
                    wait(pool, x_scaled, 2, g, i + 1)
                    xmv = by_seq(half(xm, i))
                    sh = shiftT[:, :, bass.ds(g * SEQS + i * SEQS // 2, SEQS // 2)]
                    pool.tensor_tensor(xmv, xmv, sh.unsqueeze(3).to_broadcast([P, KT, SEQS // 2, S]), ALU.add).then_inc(x_shifted, 1)
                elif name == "qk_norm":
                    wait(pool, qkv_copied, TILES, g, t + 1)
                    wait(pool, qk_rms_done, 2, g, t // 2 + 1)
                    pool.tensor_tensor(qk[:, t, 0:D], qk[:, t, 0:D], gqk[:, :], ALU.mult).then_inc(q_scaled, 1)
                    wait(pool, q_scaled, TILES, g, t + 1)
                    wait(pool, qk_turned, 2 * TILES, g, t)
                    pool.tensor_tensor(qn[:, t % 2, :].rearrange("p (h d) -> p h d", d=HD),
                                       qk[:, t, 0:D].rearrange("p (h d) -> p h d", d=HD),
                                       rqk[:, t, 0:H].unsqueeze(2).to_broadcast([P, H, HD]), ALU.mult)
                    kdst, ksrc = padded(qk[:, t, D:2 * D])
                    rk = rqk[:, t, H:2 * H].rearrange("p (a b) -> p a b", a=HP).unsqueeze(3)
                    pool.tensor_tensor(kdst, ksrc, rk.to_broadcast([P, HP, 2, HD]), ALU.mult).then_inc(qk_normed, 1)
                elif name == "o_turn":
                    wait(pool, o_turned, TILES, g, t + 1)
                    wait(pool, inverted, 2 * TILES, g, t + 1)
                    wait(pool, xT_mm, TILES, g, t + 1)
                    ri = rinv[:, t, :].rearrange("p (a b) -> p a b", a=HP).unsqueeze(3)
                    pool.tensor_tensor(tok[:, t, :].rearrange("p (a b d) -> p a b d", a=HP, b=2),
                                       own_head(oq[:, t % 2]), ri.to_broadcast([P, HP, 2, HD]),
                                       ALU.mult).then_inc(o_normed, 1)
                elif name == "p_scale":
                    n, t = i, i % TILES
                    wait(pool, inverted, 2 * TILES, g, n + 1)
                    pool.tensor_tensor(z[:, n % 2], z[:, n % 2], rinv[:, t, :].unsqueeze(2).to_broadcast([P, H, S]),
                                       ALU.mult).then_inc(scaled, 1)

            def do_ffn(name, g, i):
                c = i
                if name == "gated_split":
                    wait(pool, gh_done, FC, g, c + 1)
                    pool.tensor_tensor(gl[:, c, :], g_up[:, c % 2, :], gh[:, c, :].bitcast(F32),
                                       ALU.subtract).then_inc(gl_done, 1)

            pool.memset(rsum[:, 0, 0:1], 0.0).then_inc(gl_done, FC)
            pool.wait_ge(pads_zeroed, 3)
            run(pool, do_attention, do_ffn, lambda name, n: None)


def kernel(**inputs):
    import concourse.bacc as _bacc
    from concourse.bass_utils import run_bass_kernel_spmd as _run

    i = {k: np.asarray(v) for k, v in inputs.items()}
    q = np.arange(P) % S
    heads = (np.arange(P)[:, None] // HD == np.arange(8)[None, :]).astype(np.float32)
    causal = np.where(np.arange(S)[None, :] <= q[:, None], 0.0, -3.0e38).astype(np.float32)
    arrays = {
        "x": i["x"].reshape(B * S, D),
        "condT": i["cond_2048"].T,
        "w_emb": i["L0_cond_W_emb"],
        "b_emb": i["L0_cond_b_emb"],
        "g_norm": i["L0_cond_g_norm"],
        "w_qkv": i["L0_cond_W_qkv"],
        "gq": np.tile(i["L0_cond_g_q"], (P, H)),
        "gk": np.tile(i["L0_cond_g_k"], (P, H)),
        "w_out": i["L0_cond_W_out"],
        "ln1": i["L0_ffn_ln1_w"],
        "ln2": i["L0_ffn_ln2_w"],
        "wqT": i["L0_ffn_Wq"].T,
        "wkT": i["L0_ffn_Wk"].T,
        "wv": i["L0_ffn_Wv"],
        "wo": i["L0_ffn_Wo"],
        "a_w": i["L0_ffn_A"],
        "b_w": i["L0_ffn_B"],
        "w_inT": i["L0_ffn_W_in_base"].T,
        "w_upT": i["L0_ffn_W_up_base"].T,
        "w_downT": i["L0_ffn_W_down"].T,
        "ident": np.eye(P, dtype=np.float32),
        "heads": heads,
        "causal": causal,
    }
    nc = _bacc.Bacc("TRN2", target_bir_lowering=False, num_devices=1)
    sent, args = {}, []
    for name, a in arrays.items():
        a = np.ascontiguousarray(a)
        sent[f"in_{name}"] = a
        args.append(nc.dram_tensor(f"in_{name}", a.shape, mybir.dt.from_np(a.dtype), kind="ExternalInput").ap())
    args.append(nc.dram_tensor("out_0", (B * S, D), F32, kind="ExternalOutput").ap())
    bass_adaln_attention_ffn(nc, *args)
    r = _run(nc, [sent], core_ids=[0])
    return r.results[0]["out_0"].reshape(B, S, D)
```

```python
from contextlib import ExitStack

import numpy as np

import concourse.bass as bass
from concourse import mybir

ALU = mybir.AluOpType
ACT = mybir.ActivationFunctionType
F32 = mybir.dt.float32
F32R = mybir.dt.float32r
BF16 = mybir.dt.bfloat16
I32 = mybir.dt.int32
AX_X = mybir.AxisListType.X

P = 128
B, S, D = 128, 32, 256
H, HD = 16, 16
FF, R = 1024, 16
KT = D // P
HP = H // 2
TILES = 4
GROUP = TILES * P
GROUPS = B * S // GROUP
SEQS = GROUP // S
FC = FF // P
EPS = 1e-6
RSQRT_GUESS = float(0x5F3759DF)
NEWTON_STEPS = 3


def x_order():
    o = [("x_square", t) for t in range(TILES)] + [("x_rms", 0)] + [("x_norm", t) for t in range(TILES)]
    for q in range(2):
        o += [("x_turn", 2 * q), ("x_turn", 2 * q + 1), ("x_modulate", q), ("x_split", q)]
    return o


X_NORMS = 2 * TILES + 1


ATTENTION = [
    ("qkv_out", 0), ("qk_squares", 0), ("qkv", 0), ("qkv", 1), ("qkv_out", 1), ("qk_squares", 1),
    ("qk_rms", 0), ("qk_norm", 0), ("qk_squares", 2), ("qkv_out", 2), ("qk_turn", 0), ("qk_norm", 1),
    ("qkv", 2), ("qk_turn", 1), ("qkv", 3), ("qkv_out", 3), ("qk_squares", 3),
    ("scores", 0), ("qk_rms", 1), ("qk_norm", 2), ("shift", 0), ("exp", 0), ("scores", 1), ("shift", 1),
    ("exp", 1), ("qk_turn", 2), ("p_turn", 0), ("scores", 2), ("shift", 2), ("exp", 2), ("qk_turn", 3),
    ("qk_norm", 3), ("p_turn", 1), ("pv", 0), ("scores", 3), ("shift", 3), ("p_turn", 2), ("o_turn", 0),
    ("exp", 3), ("pv", 1), ("p_turn", 3), ("o_turn", 1), ("pv", 2), ("o_turn", 2), ("pv", 3),
    ("on_turn", 0), ("o_turn", 3), ("o_split", 0), ("on_turn", 1), ("on_turn", 2), ("on_turn", 3),
    ("o_split", 1), ("res", 0), ("res_square", 0), ("res", 1), ("res_add", 0), ("res_norm", 0),
    ("res_norm", 1), ("res", 2), ("res_rms", 0), ("res_square", 1), ("res", 3), ("res_add", 1),
    ("res_norm", 2), ("u_turn", 0), ("res_rms", 1), ("u_turn", 1), ("res_norm", 3), ("u_split", 0),
    ("u_turn", 2), ("u_turn", 3), ("u_split", 1),
    ("qkv2", 0), ("qkv2", 1), ("qkv2_out", 0), ("qk_turn", 4), ("qkv2_out", 1), ("qkv2", 2), ("qk_turn", 5),
    ("qkv2_out", 2), ("exp", 4), ("scores", 4), ("shift", 4), ("shift", 5), ("qk_turn", 6), ("scores", 5),
    ("exp", 5), ("qkv2", 3), ("qkv2_out", 3), ("scores", 6), ("p_sum", 4), ("pv", 4), ("p_turn", 4),
    ("shift", 6), ("qk_turn", 7), ("p_sum", 5), ("p_scale", 4), ("scores", 7), ("exp", 6), ("p_scale", 5),
    ("p_turn", 5), ("exp", 7), ("oa_turn", 0), ("pv", 5), ("shift", 7), ("p_scale", 6), ("p_sum", 6),
    ("p_turn", 6), ("p_sum", 7), ("oa_turn", 1), ("p_scale", 7), ("p_turn", 7), ("oa_turn", 2), ("pv", 6),
    ("pv", 7), ("oa_turn", 3),
    ("mod", 0), ("m_turn", 0), ("m_turn", 1), ("m_out", 0), ("m_turn", 2), ("m_turn", 3), ("u_copy", 0),
    ("end", 0),
]


def ffn_pieces():
    o = []
    for c in range(FC):
        o += [[("up", c)], [("gate", c)]]
        if c:
            o.append([("down", c - 1)])
        o += [[("gated", c)], [("gated_split", c)]]
    o += [[("down", FC - 1)], [("out", 0), ("out", 1)]]
    return o


FFN_AT = [("qk_squares", 1), ("qk_squares", 1), ("qk_squares", 2), ("shift", 1), ("exp", 1), ("exp", 1),
          ("exp", 2), ("p_turn", 1), ("pv", 0), ("shift", 3), ("p_turn", 2), ("p_turn", 2), ("exp", 3),
          ("pv", 1), ("pv", 3), ("on_turn", 1), ("on_turn", 2), ("on_turn", 2), ("res_add", 0),
          ("res_norm", 1), ("res_add", 1), ("u_split", 0), ("u_split", 0), ("u_turn", 2), ("u_split", 1),
          ("qkv2", 2), ("qkv2_out", 2), ("shift", 4), ("shift", 4), ("qkv2", 3), ("pv", 4), ("shift", 6),
          ("exp", 6), ("p_scale", 6), ("p_scale", 6), ("p_sum", 6), ("p_scale", 7), ("p_scale", 7),
          ("oa_turn", 2), ("u_copy", 0), ("u_copy", 0)]
X_AT = [("qkv2", 0), ("qkv2", 0), ("qkv2", 0), ("qkv2", 0), ("qkv2", 0), ("qkv2_out", 0), ("qkv2", 2),
        ("scores", 4), ("shift", 5), ("shift", 7), ("p_scale", 6), ("pv", 7), ("mod", 0), ("mod", 0),
        ("m_turn", 0), ("m_turn", 1), ("m_turn", 1)]


WEIGHTS_AT = [("qkv", 0), ("qkv_out", 2), ("qkv_out", 3), ("scores", 0), ("scores", 1), ("scores", 2),
              ("scores", 3), ("p_turn", 2), ("p_turn", 3), ("o_turn", 2), ("on_turn", 1)]


def merged(attention, others):
    out = []
    for s in attention:
        for kind, pieces, at in others:
            for piece, place in zip(pieces, at):
                if place == s:
                    out += [(kind,) + p for p in piece]
        out.append(("attention",) + s)
    return out


PIECES = [("qkv0", 768), ("qkv1", 768), ("w_out", 512), ("q2", 512), ("k2", 512), ("a2", 32),
          ("in0", 1024), ("in1", 1024), ("up0", 1024), ("up1", 1024), ("down0", 1024), ("down1", 1024),
          ("b", 1024)]


def weight_pieces():
    o = [[("piece", n)] for n in range(2, len(PIECES))]
    o[3].append(("v2", 0))
    return o


def bass_adaln_attention_ffn(nc, x, condT, w_emb, b_emb, g_norm, w_qkv, gq, gk, w_out, ln1, ln2,
                             wqT, wkT, wv, wo, a_w, b_w, w_inT, w_upT, w_downT,
                             ident_d, heads_d, causal_d, out):
    xv = x.rearrange("(g q t p) d -> g q p t d", q=2, t=2, p=P)
    outv = out.rearrange("(g q t p) d -> g q p t d", q=2, t=2, p=P)

    with ExitStack() as ctx:
        def sb(name, shape, dt=F32):
            return ctx.enter_context(nc.sbuf_tensor(name, shape, dt))

        def sem(name):
            return ctx.enter_context(nc.semaphore(name))

        wqkv = [sb(f"wqkv_{s}", [P, KT, 3 * D], F32R) for s in ("hi", "lo")]
        wres = [sb(f"wres_{s}", [P, KT, D], F32R) for s in ("hi", "lo")]
        wqkv2 = [sb(f"wqkv2_{s}", [P, KT, 3 * D + R], F32R) for s in ("hi", "lo")]
        win = [sb(f"win_{s}", [P, KT, FF], F32R) for s in ("hi", "lo")]
        wup = [sb(f"wup_{s}", [P, KT, FF], F32R) for s in ("hi", "lo")]
        wdn = [sb(f"wdn_{s}", [P, FC, D], F32R) for s in ("hi", "lo")]
        b3 = sb("b3", [96, FF], F32R)
        ident = sb("ident", [P, P])
        identb = sb("identb", [P, P], BF16)
        causal = sb("causal", [P, S])
        maskb = sb("maskb", [P, H, S], BF16)
        heads = sb("heads", [P, 8])
        small = sb("small", [P, 16])
        an = sb("an", [P, KT, R])
        gqk = sb("gqk", [P, D])
        scaleT = sb("scaleT", [P, KT, B])
        shiftT = sb("shiftT", [P, KT, B])

        x_sb = [sb(f"x{q}", [P, 2, D]) for q in range(2)]
        tok = sb("tok", [P, TILES, D])
        xm = sb("xm", [P, KT, GROUP])
        ah = sb("ah", [P, KT, GROUP], F32R)
        al = sb("al", [P, KT, GROUP], F32R)
        uh = sb("uh", [P, KT, GROUP], F32R)
        ul = sb("ul", [P, KT, GROUP], F32R)
        uf = [sb(f"uf_{s}", [P, KT, GROUP], F32R) for s in ("hi", "lo")]
        sq = sb("sq", [P, 2, 2 * D])
        qk = sb("qk", [P, TILES, 2 * D])
        vs = sb("vs", [P, TILES, D + R])
        qn = sb("qn", [P, 2, D])
        kp = sb("kp", [P, HP, 2, 2, HD])
        qT = sb("qT", [P, 2, D])
        kT = sb("kT", [P, 2, 2 * D])
        z = sb("z", [P, 2, H, S])
        pT = sb("pT", [P, 2, H * S])
        oq = sb("oq", [P, 2, HP, 4 * HD])
        mx = sb("mx", [P, 2, H])
        rsum = sb("rsum", [P, 2, H])
        rinv = sb("rinv", [P, TILES, H])
        ssx = sb("ssx", [P, TILES])
        rx = sb("rx", [P, TILES])
        ssr = sb("ssr", [P, TILES])
        rr = sb("rr", [P, TILES])
        ssq = sb("ssq", [P, TILES, 2 * H])
        rqk = sb("rqk", [P, TILES, 2 * H])
        nw_a = sb("nw_a", [P, 64])
        nw_y = sb("nw_y", [P, 64])
        nw_t = sb("nw_t", [P, 64])
        oa4 = sb("oa4", [P, TILES, 4 * HD])
        oa = sb("oa", [P, TILES, R])
        th16 = sb("th16", [P, TILES, R])
        m16 = sb("m16", [P, TILES, R])
        mt = sb("mt", [P, TILES, 96])
        mT = sb("mT", [96, GROUP], F32R)
        xres = sb("xres", [P, 2, TILES, D])
        gh = sb("gh", [P, 2, GROUP], F32R)
        gl = sb("gl", [P, 2, GROUP], F32R)
        ffn_work = sb("ffn_work", [P, 2560])
        th = ffn_work[:, 0:GROUP]
        g_up = ffn_work[:, GROUP:3 * GROUP].rearrange("p (c n) -> p c n", c=2)
        outb = ffn_work[:, 3 * GROUP:5 * GROUP].rearrange("p (t d) -> p t d", t=TILES)
        stage = ffn_work[:, 0:2048].rearrange("p (s n) -> p s n", s=2)
        we = xres[:, 1].rearrange("p t d -> p (t d)").rearrange("p (k n) -> p k n", k=KT)
        wvn = xres[:, 0, 0:2, :]
        won = xres[:, 0, 2:4, :]
        cT = xm[:, 0, 0:KT * B].rearrange("p (k n) -> p k n", k=KT)
        mblk = xres[:, 1, 0, :].rearrange("p (k h r) -> p k h r", k=KT, h=8)
        gq_sb = qk[:, 0, 0:D]
        gk_sb = qk[:, 0, D:2 * D]

        A = [ctx.enter_context(nc.psum_tensor(f"attn_bank{i}", [P, 512], F32)) for i in range(4)]
        Fb = [ctx.enter_context(nc.psum_tensor(f"ffn_bank{i}", [P, 512], F32)) for i in range(4)]

        x_loaded = [sem(f"x_loaded{q}") for q in range(2)]
        out_stored = [sem(f"out_stored{q}") for q in range(2)]
        u_copied = sem("u_copied")
        emb_loaded = sem("emb_loaded")
        v2_loaded = sem("v2_loaded")
        piece_loaded = [sem(f"piece_loaded{i}") for i in range(2)]
        piece_split = sem("piece_split")
        piece_hi = sem("piece_hi")
        emb_mm, m_mm, v2_mm = sem("emb_mm"), sem("m_mm"), sem("v2_mm")
        prep, mblk_done = sem("prep"), sem("mblk_done")
        v2_hi = sem("v2_hi")
        pads_zeroed = sem("pads_zeroed")
        x_squared, x_rms_done, x_normed, xT_mm = sem("x_squared"), sem("x_rms_done"), sem("x_normed"), sem("xT_mm")
        x_scaled, x_shifted, xh_done, xl_done = sem("x_scaled"), sem("x_shifted"), sem("xh_done"), sem("xl_done")
        qkv_mm, qk_squared, qkv_copied = sem("qkv_mm"), sem("qk_squared"), sem("qkv_copied")
        qk_summed, qk_rms_done, q_scaled, qk_normed = (sem("qk_summed"), sem("qk_rms_done"), sem("q_scaled"),
                                                       sem("qk_normed"))
        qk_turned, scores_mm, maxed, shifted, exped = (sem("qk_turned"), sem("scores_mm"), sem("maxed"),
                                                       sem("shifted"), sem("exped"))
        summed, inverted, scaled, p_turned, pv_mm = (sem("summed"), sem("inverted"), sem("scaled"),
                                                     sem("p_turned"), sem("pv_mm"))
        o_turned, o_normed, oT_mm, oh_done, ol_done = (sem("o_turned"), sem("o_normed"), sem("oT_mm"),
                                                       sem("oh_done"), sem("ol_done"))
        res_mm, res_squared, xres_done, res_rms_done, u_done = (sem("res_mm"), sem("res_squared"),
                                                                sem("xres_done"), sem("res_rms_done"), sem("u_done"))
        uT_mm, uh_done, ul_done, qkv2_mm, qkv2_copied = (sem("uT_mm"), sem("uh_done"), sem("ul_done"),
                                                         sem("qkv2_mm"), sem("qkv2_copied"))
        oa_turned, oa_summed, oa_tanh, m_done, mT_mm, mT_done = (sem("oa_turned"), sem("oa_summed"), sem("oa_tanh"),
                                                      sem("m_done"), sem("mT_mm"), sem("mT_done"))
        newton, m_chain = sem("newton"), sem("m_chain")
        gate_mm, up_mm, tanh_done, half_gated, gated_done = (sem("gate_mm"), sem("up_mm"), sem("tanh_done"),
                                                             sem("half_gated"), sem("gated_done"))
        gh_done, gl_done, down_mm, out_done = sem("gh_done"), sem("gl_done"), sem("down_mm"), sem("out_done")

        credit = [gated_done, gl_done, down_mm, out_done, *out_stored]

        def wait(eng, s, per_group, g, n):
            if any(s is c for c in credit):
                n += per_group
            if isinstance(g, int):
                if g * per_group + n > 0:
                    eng.wait_ge(s, g * per_group + n)
            else:
                eng.wait_ge(s, g * per_group + n)

        attention = ATTENTION
        x_pieces = [[p] for p in x_order()]
        steady = merged(attention, [("ffn", ffn_pieces(), FFN_AT), ("x", x_pieces, X_AT)])
        first = merged(attention, [("x", x_pieces, X_AT), ("weights", weight_pieces(), WEIGHTS_AT)])

        def run(eng, do_attention, do_ffn, do_weights, loop_starts=lambda g: None):
            for name, i in x_order()[X_NORMS:]:
                do_attention(name, 0, i)
            for kind, name, i in first:
                if kind == "weights":
                    do_weights(name, i)
                else:
                    do_attention(name, 1 if kind == "x" else 0, i)
            with eng.Fori(1, GROUPS - 1) as g:
                loop_starts(g)
                for kind, name, i in steady:
                    if kind == "ffn":
                        do_ffn(name, g - 1, i)
                    else:
                        do_attention(name, g + 1 if kind == "x" else g, i)
            loop_starts(None)
            for kind, name, i in steady:
                if kind == "ffn":
                    do_ffn(name, GROUPS - 2, i)
                elif kind == "attention":
                    do_attention(name, GROUPS - 1, i)
            for piece in ffn_pieces():
                for name, i in piece:
                    do_ffn(name, GROUPS - 1, i)

        def norms(do_attention):
            for name, i in x_order()[:X_NORMS]:
                do_attention(name, 0, i)

        piece_names = [n for n, _ in PIECES]

        def piece_parts(n):
            name = piece_names[n]
            st = stage[:, n % 2, 0:PIECES[n][1]]
            if name[:3] == "qkv":
                k = int(name[3])
                return [(st, wqkv[0][:, k, :], wqkv[1][:, k, :], 1.0)]
            if name == "w_out":
                st = st.rearrange("p (k n) -> p k n", k=KT)
                return [(st, wres[0][:, :, :], wres[1][:, :, :], 1.0)]
            if name in ("q2", "k2", "a2"):
                w = R if name == "a2" else D
                lo = {"q2": 0, "k2": D, "a2": 3 * D}[name]
                first_col = {"q2": 12, "k2": 8, "a2": 10}[name]
                st = st.rearrange("p (k n) -> p k n", k=KT)
                return [(st[:, k, :], wqkv2[0][:, k, lo:lo + w], wqkv2[1][:, k, lo:lo + w],
                         small[:, first_col + k:first_col + k + 1]) for k in range(KT)]
            if name[:2] in ("in", "up"):
                k = int(name[2])
                w = win if name[:2] == "in" else wup
                return [(st, w[0][:, k, :], w[1][:, k, :], small[:, 10 + k:11 + k])]
            if name[:4] == "down":
                k = int(name[4])
                st = st.rearrange("p (k n) -> p k n", k=FC // 2)
                sl = slice(k * FC // 2, (k + 1) * FC // 2)
                return [(st, wdn[0][:, sl, :], wdn[1][:, sl, :], 0.5)]
            return []

        def gate_up_banks(g, c):
            return A[0:2] if isinstance(g, int) and g == GROUPS - 1 and c % 2 else Fb[0:2]

        def half(buf, q):
            return buf[:, :, q * 2 * P:(q + 1) * 2 * P]

        def by_k(bank):
            return bank[:, :].rearrange("p (k n) -> p k n", k=KT)

        def by_seq(ap):
            return ap.rearrange("p k (b s) -> p k b s", s=S)

        def padded(src):
            whole = kp[:, :, :, :, :].rearrange("p a b c d -> p a (b c d)")
            dst = bass.AP(whole.tensor, whole.offset, [whole.ap[0], [4 * HD, HP], [3 * HD, 2], [1, HD]])
            return dst, src.rearrange("p (a b d) -> p a b d", a=HP, b=2)

        def own_head(src):
            return bass.AP(src.tensor, src.offset, [src.ap[0], [4 * HD, HP], [3 * HD, 2], [1, HD]])

        block = ctx.enter_context(nc.Block())

        @block.sync
        def _(sp):
            def load_x(g, q):
                wait(sp, xres_done, 2, g, q - 1)
                src = xv[bass.ds(g, 1), q].rearrange("g p t d -> p (g t) d")
                sp.dma_start(x_sb[q][:, :, :], src).then_inc(x_loaded[q], 16)

            def load_piece(n):
                if n >= 2:
                    sp.wait_ge(piece_split, n - 1)
                name = piece_names[n]
                to = piece_loaded[n % 2]
                dst = stage[:, n % 2, 0:PIECES[n][1]]
                if name == "b":
                    for j in range(3):
                        sp.dma_start(stage[32 * j:32 * j + R, n % 2, :], b_w).then_inc(to, 16)
                    return
                if name[:3] == "qkv":
                    k = int(name[3])
                    src = w_qkv[k * P:(k + 1) * P, :]
                elif name[:2] in ("in", "up"):
                    k = int(name[2])
                    src = (w_inT if name[:2] == "in" else w_upT)[k * P:(k + 1) * P, :]
                elif name[:4] == "down":
                    k = int(name[4])
                    src = w_downT[k * FF // 2:(k + 1) * FF // 2, :].rearrange("(k p) n -> p k n", p=P)
                    dst = dst.rearrange("p (k n) -> p k n", k=FC // 2)
                else:
                    w = {"w_out": w_out, "q2": wqT, "k2": wkT, "a2": a_w}[name]
                    src = w.rearrange("(k p) n -> p k n", p=P)
                    dst = dst.rearrange("p (k n) -> p k n", k=KT)
                sp.dma_start(dst, src).then_inc(to, 16)

            load_x(0, 0)
            load_x(0, 1)
            sp.dma_start(ident[:, :], ident_d).then_inc(emb_loaded, 16)
            sp.dma_start(we, w_emb.rearrange("(k p) n -> p k n", p=P)).then_inc(emb_loaded, 16)
            sp.dma_start(cT, condT.rearrange("(k p) n -> p k n", p=P)).then_inc(emb_loaded, 16)
            for col, v, n in ((0, b_emb, 4), (6, g_norm, 2), (8, ln1, 2), (10, ln2, 2)):
                with nc.allow_non_contiguous_dma(reason="vectors of features onto partitions"):
                    sp.dma_start(small[:, col:col + n], v.rearrange("(k p) -> p k", p=P)).then_inc(emb_loaded, 16)
            sp.dma_start(gq_sb, gq).then_inc(emb_loaded, 16)
            sp.dma_start(gk_sb, gk).then_inc(emb_loaded, 16)
            sp.dma_start(causal[:, :], causal_d).then_inc(emb_loaded, 16)
            load_piece(0)
            load_piece(1)
            sp.dma_start(heads[:, :], heads_d).then_inc(v2_loaded, 16)
            sp.dma_start(won, wo.rearrange("(k p) n -> p k n", p=P)).then_inc(v2_loaded, 16)
            sp.dma_start(wvn, wv.rearrange("(k p) n -> p k n", p=P)).then_inc(v2_loaded, 16)
            sp.dma_start(an[:, :, :], a_w.rearrange("(k p) n -> p k n", p=P)).then_inc(v2_loaded, 16)
            for n in range(2, len(PIECES)):
                load_piece(n)
            load_x(1, 0)
            load_x(1, 1)

            def store(g, q):
                wait(sp, out_done, 2, g, q + 1)
                dst = outv[bass.ds(g, 1), q].rearrange("g p t d -> p (g t) d")
                sp.dma_start(dst, outb[:, 2 * q:2 * q + 2, :]).then_inc(out_stored[q], 16)

            with sp.Fori(1, GROUPS - 1) as g:
                load_x(g + 1, 0)
                load_x(g + 1, 1)
                store(g - 1, 0)
                store(g - 1, 1)
            for g in (GROUPS - 2, GROUPS - 1):
                store(g, 0)
                store(g, 1)
            for q in range(2):
                sp.wait_ge(out_stored[q], 16 * (GROUPS + 1))

        @block.tensor
        def _(pe):
            def three_passes(dst, stat, mov, first_mm, last_mm):
                for j, (a, b) in enumerate(((0, 0), (0, 1), (1, 0))):
                    mm = pe.matmul(dst, stat[a], mov[b], start=first_mm and j == 0, stop=last_mm and j == 2)
                return mm

            def token_major(dsts, stat_hi, stat_lo, w, cols, t):
                for k in range(KT):
                    for j, (a, b) in enumerate(((stat_hi, 0), (stat_hi, 1), (stat_lo, 0))):
                        for dst, (c0, c1) in zip(dsts, cols):
                            mm = pe.matmul(dst, a[:, k, t * P:(t + 1) * P], w[b][:, k, c0:c1],
                                           start=(k == 0 and j == 0), stop=(k == KT - 1 and j == 2))
                return mm

            def turn(bank, t):
                for k in range(KT):
                    c = (k * 2 + t % 2) * P
                    mm = pe.transpose(bank[:, c:c + P], tok[:, t, k * P:(k + 1) * P], ident[:, :])
                return mm

            def do_attention(name, g, i):
                t = i
                if name == "x_turn":
                    wait(pe, x_normed, TILES, g, t + 1)
                    if t % 2 == 0:
                        wait(pe, oa_turned, TILES, g, t // 2 + 1 - TILES)
                    turn(A[t // 2], t).then_inc(xT_mm, 1)
                elif name == "qkv":
                    if t % 2 == 0:
                        wait(pe, xl_done, 2, g, t // 2 + 1)
                    if t == 0:
                        wait(pe, x_scaled, 2, g, 2)
                    elif t == 1:
                        wait(pe, oa_turned, TILES, g, 0)
                        wait(pe, mT_done, 1, g, 0)
                    else:
                        wait(pe, qkv_copied, TILES, g, t - 1)
                    if isinstance(g, int) and t == 0:
                        pe.wait_ge(piece_split, 2)
                    pair = 2 * (t % 2)
                    token_major([A[pair][:, :], A[pair + 1][:, 0:D]], ah, al, wqkv, [(0, 512), (512, 768)],
                                t).then_inc(qkv_mm, 1)
                elif name == "scores":
                    n, second = i, i >= TILES
                    t = n % TILES
                    wait(pe, qk_turned, 2 * TILES, g, n + 1)
                    pair_reader = 2 if t < 2 else 3
                    wait(pe, qkv2_copied if second else qkv_copied, TILES, g, pair_reader + 1)
                    if second:
                        pe.matmul(A[t][:, :], identb[:, :], maskb[:, :, :].rearrange("p h s -> p (h s)"),
                                  start=True, stop=False, skip_group_check=True)
                    for hp in range(HP):
                        for b in range(4):
                            rows = slice(32 * b, 32 * b + 32)
                            wide = 32 * (not second and hp + b == 0)
                            dst = slice(32 * b, 32 * b + 32 + wide)
                            mm = pe.matmul(A[t][dst, 64 * hp:64 * hp + 64], qT[rows, n % 2, 32 * hp:32 * hp + 32 + wide],
                                           kT[rows, n % 2, 64 * hp:64 * hp + 64], start=not second, stop=True,
                                           skip_group_check=True)
                    mm.then_inc(scores_mm, 1)
                elif name == "pv":
                    n, second = i, i >= TILES
                    t = n % TILES
                    wait(pe, p_turned, 2 * TILES, g, n + 1)
                    for hp in range(HP):
                        for b in range(4):
                            rows = slice(32 * b, 32 * b + 32)
                            wide = 32 * (hp + b == 0)
                            out_rows = slice(32 * b, 32 * b + 32 + wide)
                            dst = A[t][out_rows, 0:64] if second else A[t][out_rows, 64 * hp:64 * hp + 64]
                            mm = pe.matmul(dst, vs[rows, t, 32 * hp:32 * hp + 32 + wide],
                                           pT[rows, n % 2, 64 * hp:64 * hp + 64],
                                           start=(not second or hp == 0), stop=(not second or hp == HP - 1),
                                           skip_group_check=True)
                    mm.then_inc(pv_mm, 1)
                elif name == "on_turn":
                    wait(pe, o_normed, TILES, g, t + 1)
                    if t % 2 == 0:
                        wait(pe, o_turned, TILES, g, t // 2 + 1)
                    turn(A[t // 2], t).then_inc(oT_mm, 1)
                elif name == "res":
                    if t % 2 == 0:
                        wait(pe, ol_done, 2, g, t // 2 + 1)
                    if t == 0:
                        wait(pe, o_turned, TILES, g, TILES)
                        if isinstance(g, int):
                            pe.wait_ge(piece_split, 3)
                    dst = A[2 + t // 2][:, (t % 2) * D:(t % 2 + 1) * D]
                    token_major([dst], ah, al, wres, [(0, D)], t).then_inc(res_mm, 1)
                elif name == "u_turn":
                    wait(pe, u_done, TILES, g, t + 1)
                    if t % 2 == 0:
                        wait(pe, ol_done, 2, g, t // 2 + 1)
                    turn(A[t // 2], t).then_inc(uT_mm, 1)
                elif name == "qkv2":
                    if t % 2 == 0:
                        wait(pe, ul_done, 2, g, t // 2 + 1)
                    if t == 0:
                        wait(pe, ul_done, 2, g, 2)
                        if isinstance(g, int):
                            pe.wait_ge(piece_split, 6)
                            pe.wait_ge(v2_hi, 2)
                    elif t == 1:
                        wait(pe, u_done, TILES, g, TILES)
                    else:
                        wait(pe, qkv2_copied, TILES, g, t - 1)
                    pair = 2 * (t % 2)
                    token_major([A[pair][:, :], A[pair + 1][:, 0:D + R]], uh, ul, wqkv2,
                                [(0, 512), (512, 768 + R)], t).then_inc(qkv2_mm, 1)
                elif name == "m_turn":
                    if t == 0:
                        wait(pe, m_done, 1, g, 1)
                        wait(pe, oa_turned, TILES, g, TILES)
                    pe.transpose(A[2][0:96, t * P:(t + 1) * P], mt[:, t, :], ident[:, :]).then_inc(mT_mm, 1)

            def do_ffn(name, g, i):
                c = i
                if name in ("gate", "up"):
                    bank = gate_up_banks(g, c)[int(name == "up")]
                    w = win if name == "gate" else wup
                    two_pairs = isinstance(g, int) and g == GROUPS - 1
                    wait(pe, gated_done, FC, g, max(c - 1, 0) if two_pairs else c)
                    if name == "up" and c == 0:
                        wait(pe, u_copied, 1, g, 1)
                    fs = slice(c * P, (c + 1) * P)
                    for k in range(KT):
                        mm = three_passes(bank[:, :], (w[0][:, k, fs], w[1][:, k, fs]), (uf[0][:, k, :], uf[1][:, k, :]),
                                          k == 0, name == "up" and k == KT - 1)
                    if name == "gate":
                        if c == 0:
                            wait(pe, mT_done, 1, g, 1)
                        mm = pe.matmul(bank[:, :], b3[:, c * P:(c + 1) * P], mT[:, :], start=False, stop=True)
                        mm.then_inc(gate_mm, 1)
                    else:
                        mm.then_inc(up_mm, 1)
                elif name == "down":
                    wait(pe, gl_done, FC, g, c + 1)
                    if c == 0:
                        wait(pe, out_done, 2, g, 0)
                    for t in range(TILES):
                        dst = Fb[2 + t // 2][:, (t % 2) * D:(t % 2 + 1) * D]
                        stat = (gh[:, c % 2, t * P:(t + 1) * P], gl[:, c % 2, t * P:(t + 1) * P])
                        for j, (a, b) in enumerate(((0, 0), (0, 1), (1, 0))):
                            mm = pe.matmul(dst, stat[a], wdn[b][:, c, :], start=(c == 0 and t % 2 == 0 and j == 0),
                                           stop=(c == FC - 1 and j == 2), skip_group_check=True)
                    mm.then_inc(down_mm, 1)

            def do_weights(name, n):
                if name == "piece" and piece_names[n] == "w_out":
                    pe.wait_ge(v2_loaded, 64)
                    pe.wait_ge(pads_zeroed, 3)
                    for m in range(KT):
                        for k in range(KT):
                            mm = pe.matmul(Fb[3][:, m * R:(m + 1) * R], won[:, k, m * P:(m + 1) * P], an[:, k, :],
                                           start=(k == 0), stop=(k == KT - 1))
                    mm.then_inc(m_mm, 1)
                elif name == "v2":
                    pe.wait_ge(mblk_done, 1)
                    for f in range(KT):
                        for m in range(KT):
                            mm = pe.matmul(Fb[2][:, f * D + m * P:f * D + (m + 1) * P],
                                           wvn[:, m, f * P:(f + 1) * P],
                                           mblk[:, m, :, :].rearrange("p h r -> p (h r)"), start=True, stop=True)
                    mm.then_inc(v2_mm, 1)

            pe.wait_ge(emb_loaded, 16 * 10)
            for m in range(4):
                for k in range(KT):
                    mm = pe.matmul(Fb[3][:, m * B:(m + 1) * B], we[:, k, m * P:(m + 1) * P], cT[:, k, :],
                                   start=(k == 0), stop=(k == KT - 1))
                if m == 0:
                    mm.then_inc(down_mm, FC)
            mm.then_inc(emb_mm, 1)
            run(pe, do_attention, do_ffn, do_weights)

        @block.scalar
        def _(act):
            def do_attention(name, g, i):
                t = i
                if name == "x_square":
                    wait(act, x_loaded[t // 2], 16, g, 16)
                    wait(act, uT_mm, TILES, g, t - 3)
                    act.activation(tok[:, t, :], x_sb[t // 2][:, t % 2, :], ACT.Square,
                                   accum_out=ssx[:, t:t + 1]).then_inc(x_squared, 1)
                elif name == "x_norm":
                    wait(act, x_rms_done, 1, g, 1)
                    act.activation(tok[:, t, :], x_sb[t // 2][:, t % 2, :], ACT.Copy,
                                   scale=rx[:, t:t + 1]).then_inc(x_normed, 1)
                elif name == "x_split":
                    wait(act, x_shifted, 2, g, i + 1)
                    wait(act, res_mm, TILES, g, 0)
                    act.activation(half(ah, i), half(xm, i), ACT.Copy).then_inc(xh_done, 1)
                elif name == "qkv_out":
                    pair = 2 * (t % 2)
                    wait(act, qkv_mm, TILES, g, t + 1)
                    wait(act, qk_summed, TILES, g, t - 1)
                    act.activation(sq[:, t % 2, :], A[pair][:, :], ACT.Square).then_inc(qk_squared, 1)
                    wait(act, qk_normed, TILES, g, t - 3)
                    act.activation(qk[:, t, :], A[pair][:, :], ACT.Copy)
                    wait(act, pv_mm, 2 * TILES, g, t - 3)
                    act.activation(vs[:, t, 0:D], A[pair + 1][:, 0:D], ACT.Copy).then_inc(qkv_copied, 1)
                elif name == "exp":
                    wait(act, shifted, 2 * TILES, g, i + 1)
                    act.activation(z[:, i % 2], z[:, i % 2], ACT.Exp).then_inc(exped, 1)
                elif name == "o_split":
                    wait(act, oT_mm, TILES, g, 2 * i + 2)
                    wait(act, qkv_mm, TILES, g, TILES)
                    act.activation(half(ah, i), by_k(A[i]), ACT.Copy).then_inc(oh_done, 1)
                elif name == "res_square":
                    for t in (2 * i, 2 * i + 1):
                        wait(act, res_mm, TILES, g, 2 * i + 2)
                        act.activation(tok[:, t, :], A[2 + i][:, (t % 2) * D:(t % 2 + 1) * D], ACT.Square,
                                       accum_out=ssr[:, t:t + 1]).then_inc(res_squared, 1)
                elif name == "res_norm":
                    wait(act, res_rms_done, 2, g, t // 2 + 1)
                    act.activation(tok[:, t, :], A[2 + t // 2][:, (t % 2) * D:(t % 2 + 1) * D], ACT.Copy,
                                   scale=rr[:, t:t + 1]).then_inc(u_done, 1)
                elif name == "u_split":
                    wait(act, uT_mm, TILES, g, 2 * i + 2)
                    act.activation(half(uh, i), by_k(A[i]), ACT.Copy).then_inc(uh_done, 1)
                elif name == "qkv2_out":
                    n = TILES + t
                    pair = 2 * (t % 2)
                    wait(act, qkv2_mm, TILES, g, t + 1)
                    wait(act, qk_turned, 2 * TILES, g, n - 1)
                    act.activation(qn[:, n % 2, :], A[pair][:, 0:D], ACT.Copy)
                    wait(act, qk_turned, 2 * TILES, g, n)
                    kdst, ksrc = padded(A[pair][:, D:2 * D])
                    act.activation(kdst, ksrc, ACT.Copy)
                    wait(act, pv_mm, 2 * TILES, g, t + 1)
                    act.activation(vs[:, t, :], A[pair + 1][:, 0:D + R], ACT.Copy).then_inc(qkv2_copied, 1)
                elif name == "mod":
                    wait(act, oa_summed, TILES, g, TILES)
                    act.activation(th16[:, :, :], oa[:, :, :], ACT.Tanh).then_inc(oa_tanh, 1)
                elif name == "m_out":
                    wait(act, mT_mm, TILES, g, TILES)
                    wait(act, gate_mm, FC, g, 0)
                    act.activation(mT[:, :], A[2][0:96, :], ACT.Copy).then_inc(mT_done, 1)
                elif name == "u_copy":
                    wait(act, ul_done, 2, g, 2)
                    wait(act, gate_mm, FC, g, 0)
                    act.activation(uf[0][:, :, :], uh[:, :, :], ACT.Copy)
                    act.activation(uf[1][:, :, :], ul[:, :, :], ACT.Copy).then_inc(u_copied, 1)

            def do_ffn(name, g, i):
                c = i
                if name == "gate":
                    wait(act, gate_mm, FC, g, c + 1)
                    wait(act, gated_done, FC, g, c)
                    act.activation(th, gate_up_banks(g, c)[0][:, :], ACT.Tanh, scale=0.5).then_inc(tanh_done, 1)
                elif name == "gated_split":
                    wait(act, gated_done, FC, g, c + 1)
                    wait(act, down_mm, FC, g, max(c - 1, 0))
                    act.activation(gh[:, c % 2, :], g_up[:, c % 2, :], ACT.Copy).then_inc(gh_done, 1)

            def do_weights(name, n):
                if name == "v2":
                    act.wait_ge(v2_mm, 1)
                    for k in range(KT):
                        hi = act.activation(wqkv2[0][:, k, 512:768], Fb[2][:, k * D:(k + 1) * D], ACT.Copy,
                                            scale=small[:, 8 + k:9 + k])
                    hi.then_inc(v2_hi, 1)
                    return
                if piece_names[n] == "b":
                    return
                act.wait_ge(piece_loaded[n % 2], 16 * (n // 2 + 1))
                if piece_names[n] == "w_out":
                    act.wait_ge(prep, 3)
                for st, hi_ap, _, scale in piece_parts(n):
                    hi = act.activation(hi_ap, st, ACT.Copy, scale=scale)
                hi.then_inc(piece_hi, 1)

            norms(do_attention)
            do_weights("piece", 0)
            do_weights("piece", 1)
            act.wait_ge(prep, 2)
            run(act, do_attention, do_ffn, do_weights)

        @block.vector
        def _(dve):
            count = {"steps": 0, "ahead": 0, "per_pass": 0, "passes": 0}

            def loop_starts(g):
                if g is None:
                    count.update(steps=count["ahead"] + (GROUPS - 2) * count["per_pass"], ahead=0, passes=0)
                else:
                    count.update(ahead=count["steps"], per_pass=count["steps"] - count["adaln"], steps=0,
                                 passes=g - 1)

            def rsqrt(dst, src, n, g, signal):
                w = dst.shape[-1] if len(dst.shape) == 2 else dst.shape[-1] * dst.shape[-2]
                a, y, u = nw_a[:, 0:w], nw_y[:, 0:w], nw_t[:, 0:w]
                base = count["ahead"] + count["passes"] * count["per_pass"]

                def then(ins):
                    count["steps"] += 1
                    ins.then_inc(newton, 1)
                    dve.wait_ge(newton, base + count["steps"])

                then(dve.tensor_scalar(a, src, 1.0 / n, EPS, ALU.mult, ALU.add))
                then(dve.tensor_scalar(y.bitcast(I32), a.bitcast(I32), 1, None, ALU.arith_shift_right))
                then(dve.tensor_scalar(y.bitcast(I32), y.bitcast(I32), -1, RSQRT_GUESS, ALU.mult, ALU.add))
                for s in range(NEWTON_STEPS):
                    then(dve.scalar_tensor_tensor(out=u, in0=y, scalar=-0.5, in1=y, op0=ALU.mult, op1=ALU.mult))
                    then(dve.tensor_tensor(u, u, a, ALU.mult))
                    if s < NEWTON_STEPS - 1:
                        then(dve.scalar_tensor_tensor(out=y, in0=u, scalar=1.5, in1=y, op0=ALU.add, op1=ALU.mult))
                dve.scalar_tensor_tensor(out=dst, in0=u, scalar=1.5, in1=y, op0=ALU.add,
                                         op1=ALU.mult).then_inc(signal, 1)

            def do_attention(name, g, i):
                t = i
                if name == "x_rms":
                    wait(dve, x_squared, TILES, g, TILES)
                    rsqrt(rx[:, :], ssx[:, :], D, g, x_rms_done)
                elif name == "x_modulate":
                    wait(dve, xT_mm, TILES, g, 2 * i + 2)
                    wait(dve, xh_done, 2, g, i - 1)
                    sc = scaleT[:, :, bass.ds(g * SEQS + i * SEQS // 2, SEQS // 2)]
                    dve.tensor_tensor(by_seq(half(xm, i)), by_seq(by_k(A[i])),
                                      sc.unsqueeze(3).to_broadcast([P, KT, SEQS // 2, S]),
                                      ALU.mult).then_inc(x_scaled, 1)
                elif name == "x_split":
                    if isinstance(g, int) and g == 0:
                        count["adaln"] = count["steps"]
                    wait(dve, xh_done, 2, g, i + 1)
                    dve.tensor_tensor(half(al, i), half(xm, i), half(ah, i).bitcast(F32),
                                      ALU.subtract).then_inc(xl_done, 1)
                elif name == "qk_squares":
                    wait(dve, qk_squared, TILES, g, t + 1)
                    wait(dve, qk_rms_done, 2, g, t // 2 - 1)
                    dve.tensor_reduce(ssq[:, t, :], sq[:, t % 2, :].rearrange("p (h d) -> p h d", d=HD), AX_X,
                                      ALU.add).then_inc(qk_summed, 1)
                elif name == "qk_rms":
                    wait(dve, qk_summed, TILES, g, 2 * i + 2)
                    wait(dve, qk_normed, TILES, g, 2 * i - 2)
                    rsqrt(rqk[:, 2 * i:2 * i + 2, :].rearrange("p t h -> p (t h)"),
                          ssq[:, 2 * i:2 * i + 2, :].rearrange("p t h -> p (t h)"), HD, g, qk_rms_done)
                elif name == "qk_turn":
                    n = i
                    if n < TILES:
                        wait(dve, qk_normed, TILES, g, n + 1)
                    else:
                        wait(dve, qkv2_copied, TILES, g, n - TILES + 1)
                    wait(dve, scores_mm, 2 * TILES, g, n - 1)
                    dve.transpose(qT[:, n % 2, :], qn[:, n % 2, :])
                    dve.transpose(kT[:, n % 2, :],
                                  kp[:, :, :, :, :].rearrange("p a b c d -> p (a b c d)")).then_inc(qk_turned, 1)
                elif name == "shift":
                    n, t = i, i % TILES
                    wait(dve, scores_mm, 2 * TILES, g, n + 1)
                    sc = A[t][:, :].rearrange("p (h s) -> p h s", s=S)
                    dve.tensor_reduce(mx[:, n % 2, :], sc, AX_X, ALU.max).then_inc(maxed, 1)
                    wait(dve, maxed, 2 * TILES, g, n + 1)
                    wait(dve, p_turned, 2 * TILES, g, n - 1)
                    dve.tensor_tensor(z[:, n % 2], sc, mx[:, n % 2, :].unsqueeze(2).to_broadcast([P, H, S]),
                                      ALU.subtract).then_inc(shifted, 1)
                elif name in ("p_sum", "p_turn"):
                    n, t = i, i % TILES
                    if name == "p_sum" or n < TILES:
                        wait(dve, exped, 2 * TILES, g, n + 1)
                        wait(dve, inverted, 2 * TILES, g, n)
                        dve.tensor_reduce(rsum[:, n % 2, :], z[:, n % 2], AX_X, ALU.add).then_inc(summed, 1)
                        wait(dve, summed, 2 * TILES, g, n + 1)
                        wait(dve, o_normed if n >= TILES else scaled, TILES, g, t + 1 if n >= TILES else t - 3)
                        dve.reciprocal(rinv[:, t, :], rsum[:, n % 2, :]).then_inc(inverted, 1)
                    if name == "p_turn":
                        if n >= TILES:
                            wait(dve, scaled, TILES, g, t + 1)
                        wait(dve, pv_mm, 2 * TILES, g, n - 1)
                        dve.transpose(pT[:, n % 2, :],
                                      z[:, n % 2].rearrange("p h s -> p (h s)")).then_inc(p_turned, 1)
                elif name == "o_turn":
                    wait(dve, pv_mm, 2 * TILES, g, t + 1)
                    wait(dve, o_normed, TILES, g, t - 1)
                    dve.transpose(oq[:, t % 2].rearrange("p a b -> p (a b)"), A[t][:, :]).then_inc(o_turned, 1)
                elif name == "o_split":
                    wait(dve, oh_done, 2, g, i + 1)
                    dve.tensor_tensor(half(al, i), by_k(A[i]), half(ah, i).bitcast(F32),
                                      ALU.subtract).then_inc(ol_done, 1)
                elif name == "res_add":
                    wait(dve, res_squared, TILES, g, 2 * i + 2)
                    wait(dve, out_done, 2, g, -2)
                    dst = xres[:, bass.ds(g % 2, 1), 2 * i:2 * i + 2, :].rearrange("p g t d -> p (g t) d")
                    dve.tensor_tensor(dst, A[2 + i][:, :].rearrange("p (t d) -> p t d", t=2), x_sb[i][:, :, :],
                                      ALU.add).then_inc(xres_done, 1)
                elif name == "res_rms":
                    rsqrt(rr[:, 2 * i:2 * i + 2], ssr[:, 2 * i:2 * i + 2], D, g, res_rms_done)
                elif name == "u_split":
                    wait(dve, uh_done, 2, g, i + 1)
                    dve.tensor_tensor(half(ul, i), by_k(A[i]), half(uh, i).bitcast(F32),
                                      ALU.subtract).then_inc(ul_done, 1)
                elif name == "oa_turn":
                    wait(dve, pv_mm, 2 * TILES, g, TILES + t + 1)
                    dve.transpose(oa4[:, t, :], A[t][:, 0:64]).then_inc(oa_turned, 1)
                    wait(dve, oa_turned, TILES, g, t + 1)
                    ins = dve.tensor_tensor(oa[:, t, :], oa4[:, t, 0:HD], oa4[:, t, 3 * HD:4 * HD], ALU.add)
                    ins.then_inc(oa_summed, 1)
                elif name == "mod":
                    wait(dve, oa_tanh, 1, g, 1)
                    wait(dve, mT_mm, TILES, g, 0)
                    dve.scalar_tensor_tensor(out=m16[:, :, :], in0=th16[:, :, :], scalar=0.1,
                                             in1=vs[:, :, D:D + R], op0=ALU.mult, op1=ALU.mult).then_inc(m_chain, 1)
                    wait(dve, m_chain, 2, g, 1)
                    dve.tensor_copy(mt[:, :, 0:R].bitcast(F32R), m16[:, :, :])
                    dve.tensor_copy(mt[:, :, 64:64 + R].bitcast(F32R), m16[:, :, :]).then_inc(m_chain, 1)
                    wait(dve, m_chain, 2, g, 2)
                    dve.tensor_tensor(mt[:, :, 32:32 + R], m16[:, :, :], mt[:, :, 64:64 + R],
                                      ALU.subtract).then_inc(m_done, 1)

            def do_ffn(name, g, i):
                c = i
                if name == "gated":
                    wait(dve, tanh_done, FC, g, c + 1)
                    dve.scalar_tensor_tensor(out=th, in0=th, scalar=1.0, in1=gate_up_banks(g, c)[0][:, :], op0=ALU.add,
                                             op1=ALU.mult).then_inc(half_gated, 1)
                    wait(dve, half_gated, FC, g, c + 1)
                    wait(dve, up_mm, FC, g, c + 1)
                    wait(dve, gl_done, FC, g, max(c - 1, 0))
                    dve.tensor_tensor(g_up[:, c % 2, :], th, gate_up_banks(g, c)[1][:, :],
                                      ALU.mult).then_inc(gated_done, 1)
                elif name == "out":
                    q = i
                    wait(dve, down_mm, FC, g, FC)
                    wait(dve, out_stored[q], 16, g, 0)
                    wait(dve, xres_done, 2, g, 2)
                    src = xres[:, bass.ds(g % 2, 1), 2 * q:2 * q + 2, :].rearrange("p g t d -> p (g t) d")
                    dve.tensor_tensor(outb[:, 2 * q:2 * q + 2, :], Fb[2 + q][:, :].rearrange("p (t d) -> p t d", t=2),
                                      src, ALU.add).then_inc(out_done, 1)

            def do_weights(name, n):
                if name == "v2":
                    dve.wait_ge(v2_hi, 1)
                    for k in range(KT):
                        lo = dve.scalar_tensor_tensor(out=wqkv2[1][:, k, 512:768], in0=Fb[2][:, k * D:(k + 1) * D],
                                                      scalar=small[:, 8 + k:9 + k],
                                                      in1=wqkv2[0][:, k, 512:768].bitcast(F32),
                                                      op0=ALU.mult, op1=ALU.subtract)
                    lo.then_inc(v2_hi, 1)
                    return
                name = piece_names[n]
                if name == "b":
                    dve.wait_ge(piece_loaded[n % 2], 16 * (n // 2 + 3))
                    dve.wait_ge(pads_zeroed, 2)
                    for j in range(3):
                        rows = slice(32 * j, 32 * j + R)
                        ins = dve.tensor_copy(b3[rows, :], stage[rows, n % 2, :])
                    ins.then_inc(prep, 1)
                    dve.wait_ge(prep, 4)
                    dve.tensor_tensor(b3[64:64 + R, :], stage[64:64 + R, n % 2, :], b3[64:64 + R, :].bitcast(F32),
                                      ALU.subtract).then_inc(piece_split, 1)
                    return
                if name == "w_out":
                    dve.wait_ge(m_mm, 1)
                    for m in range(KT):
                        mb = dve.tensor_tensor(mblk[:, m], Fb[3][:, m * R:(m + 1) * R].unsqueeze(1).to_broadcast([P, 8, R]),
                                               heads[:, :].unsqueeze(2).to_broadcast([P, 8, R]), ALU.mult)
                    mb.then_inc(mblk_done, 1)
                    dve.wait_ge(piece_loaded[n % 2], 16 * (n // 2 + 1))
                    for k in range(KT):
                        seg = stage[:, n % 2, k * D + k * P:k * D + (k + 1) * P]
                        ins = dve.tensor_tensor(seg, seg, ident[:, :], ALU.add)
                    ins.then_inc(prep, 1)
                dve.wait_ge(piece_hi, n + 1)
                parts = piece_parts(n)
                for j, (st, hi_ap, lo_ap, scale) in enumerate(parts):
                    ins = dve.scalar_tensor_tensor(out=lo_ap, in0=st, scalar=scale, in1=hi_ap.bitcast(F32),
                                                   op0=ALU.mult, op1=ALU.subtract)
                ins.then_inc(piece_split, 1)

            dve.memset(kp[:, :, :, :, :], 0.0).then_inc(gated_done, FC)
            for q in range(2):
                dve.memset(mx[:, 0, q:q + 1], 0.0).then_inc(out_stored[q], 16)
            dve.memset(mx[:, 0, 2:3], 0.0).then_inc(out_done, 2)
            dve.memset(mt[:, :, :], 0.0).then_inc(pads_zeroed, 1)
            dve.memset(b3[:, :].bitcast(F32), 0.0).then_inc(pads_zeroed, 1)
            norms(do_attention)
            dve.wait_ge(emb_loaded, 16 * 10)
            dve.tensor_scalar(small[:, 12:14], small[:, 8:10], 0.25, None, ALU.mult)
            dve.tensor_scalar(small[:, 4:6], small[:, 0:2], 1.0, None, ALU.add).then_inc(prep, 1)
            dve.tensor_copy(identb[:, :], ident[:, :])
            dve.tensor_copy(maskb[:, :, :], causal[:, :].unsqueeze(1).to_broadcast([P, H, S]))
            dve.scalar_tensor_tensor(out=gqk[:, :], in0=gq_sb, scalar=float(HD) ** -0.5, in1=gk_sb,
                                     op0=ALU.mult, op1=ALU.mult).then_inc(prep, 1)
            dve.wait_ge(emb_mm, 1)
            dve.wait_ge(prep, 2)
            for k in range(KT):
                dve.tensor_scalar(scaleT[:, k, :], Fb[3][:, k * B:(k + 1) * B], small[:, 4 + k:5 + k],
                                  small[:, 6 + k:7 + k], ALU.add, ALU.mult)
                ins = dve.tensor_scalar(shiftT[:, k, :], Fb[3][:, (2 + k) * B:(3 + k) * B], small[:, 2 + k:3 + k],
                                        None, ALU.add)
            ins.then_inc(pads_zeroed, 1)
            dve.wait_ge(pads_zeroed, 3)
            do_weights("piece", 0)
            do_weights("piece", 1)
            run(dve, do_attention, do_ffn, do_weights, loop_starts)

        @block.gpsimd
        def _(pool):
            def do_attention(name, g, i):
                t = i
                if name == "x_modulate":
                    wait(pool, x_scaled, 2, g, i + 1)
                    xmv = by_seq(half(xm, i))
                    sh = shiftT[:, :, bass.ds(g * SEQS + i * SEQS // 2, SEQS // 2)]
                    pool.tensor_tensor(xmv, xmv, sh.unsqueeze(3).to_broadcast([P, KT, SEQS // 2, S]), ALU.add).then_inc(x_shifted, 1)
                elif name == "qk_norm":
                    wait(pool, qkv_copied, TILES, g, t + 1)
                    wait(pool, qk_rms_done, 2, g, t // 2 + 1)
                    pool.tensor_tensor(qk[:, t, 0:D], qk[:, t, 0:D], gqk[:, :], ALU.mult).then_inc(q_scaled, 1)
                    wait(pool, q_scaled, TILES, g, t + 1)
                    wait(pool, qk_turned, 2 * TILES, g, t)
                    pool.tensor_tensor(qn[:, t % 2, :].rearrange("p (h d) -> p h d", d=HD),
                                       qk[:, t, 0:D].rearrange("p (h d) -> p h d", d=HD),
                                       rqk[:, t, 0:H].unsqueeze(2).to_broadcast([P, H, HD]), ALU.mult)
                    kdst, ksrc = padded(qk[:, t, D:2 * D])
                    rk = rqk[:, t, H:2 * H].rearrange("p (a b) -> p a b", a=HP).unsqueeze(3)
                    pool.tensor_tensor(kdst, ksrc, rk.to_broadcast([P, HP, 2, HD]), ALU.mult).then_inc(qk_normed, 1)
                elif name == "o_turn":
                    wait(pool, o_turned, TILES, g, t + 1)
                    wait(pool, inverted, 2 * TILES, g, t + 1)
                    wait(pool, xT_mm, TILES, g, t + 1)
                    ri = rinv[:, t, :].rearrange("p (a b) -> p a b", a=HP).unsqueeze(3)
                    pool.tensor_tensor(tok[:, t, :].rearrange("p (a b d) -> p a b d", a=HP, b=2),
                                       own_head(oq[:, t % 2]), ri.to_broadcast([P, HP, 2, HD]),
                                       ALU.mult).then_inc(o_normed, 1)
                elif name == "p_scale":
                    n, t = i, i % TILES
                    wait(pool, inverted, 2 * TILES, g, n + 1)
                    pool.tensor_tensor(z[:, n % 2], z[:, n % 2], rinv[:, t, :].unsqueeze(2).to_broadcast([P, H, S]),
                                       ALU.mult).then_inc(scaled, 1)

            def do_ffn(name, g, i):
                c = i
                if name == "gated_split":
                    wait(pool, gh_done, FC, g, c + 1)
                    pool.tensor_tensor(gl[:, c % 2, :], g_up[:, c % 2, :], gh[:, c % 2, :].bitcast(F32),
                                       ALU.subtract).then_inc(gl_done, 1)

            pool.memset(rsum[:, 0, 0:1], 0.0).then_inc(gl_done, FC)
            pool.wait_ge(pads_zeroed, 3)
            run(pool, do_attention, do_ffn, lambda name, n: None)


def kernel(**inputs):
    import concourse.bacc as _bacc
    from concourse.bass_utils import run_bass_kernel_spmd as _run

    i = {k: np.asarray(v) for k, v in inputs.items()}
    q = np.arange(P) % S
    heads = (np.arange(P)[:, None] // HD == np.arange(8)[None, :]).astype(np.float32)
    causal = np.where(np.arange(S)[None, :] <= q[:, None], 0.0, -3.0e38).astype(np.float32)
    arrays = {
        "x": i["x"].reshape(B * S, D),
        "condT": i["cond_2048"].T,
        "w_emb": i["L0_cond_W_emb"],
        "b_emb": i["L0_cond_b_emb"],
        "g_norm": i["L0_cond_g_norm"],
        "w_qkv": i["L0_cond_W_qkv"],
        "gq": np.tile(i["L0_cond_g_q"], (P, H)),
        "gk": np.tile(i["L0_cond_g_k"], (P, H)),
        "w_out": i["L0_cond_W_out"],
        "ln1": i["L0_ffn_ln1_w"],
        "ln2": i["L0_ffn_ln2_w"],
        "wqT": i["L0_ffn_Wq"].T,
        "wkT": i["L0_ffn_Wk"].T,
        "wv": i["L0_ffn_Wv"],
        "wo": i["L0_ffn_Wo"],
        "a_w": i["L0_ffn_A"],
        "b_w": i["L0_ffn_B"],
        "w_inT": i["L0_ffn_W_in_base"].T,
        "w_upT": i["L0_ffn_W_up_base"].T,
        "w_downT": i["L0_ffn_W_down"].T,
        "ident": np.eye(P, dtype=np.float32),
        "heads": heads,
        "causal": causal,
    }
    nc = _bacc.Bacc("TRN2", target_bir_lowering=False, num_devices=1)
    sent, args = {}, []
    for name, a in arrays.items():
        a = np.ascontiguousarray(a)
        sent[f"in_{name}"] = a
        args.append(nc.dram_tensor(f"in_{name}", a.shape, mybir.dt.from_np(a.dtype), kind="ExternalInput").ap())
    args.append(nc.dram_tensor("out_0", (B * S, D), F32, kind="ExternalOutput").ap())
    bass_adaln_attention_ffn(nc, *args)
    r = _run(nc, [sent], core_ids=[0])
    return r.results[0]["out_0"].reshape(B, S, D)
```
